# Optimizing a Trainium2 kernel written in Bass

```python
import numpy as np
import jax
import jax.numpy as jnp

def _softmax(x, axis=-1):
    return jax.nn.softmax(x, axis=axis)

def _gelu(x):
    return jax.nn.gelu(x, approximate=True)

def _silu(x):
    return jax.nn.silu(x)

def _sigmoid(x):
    return jax.nn.sigmoid(x)

def _layernorm(x, axis=-1, eps=1e-05):
    m = jnp.mean(x, axis=axis, keepdims=True)
    v = jnp.var(x, axis=axis, keepdims=True)
    return (x - m) / jnp.sqrt(v + eps)

def _scatter_add(tgt, idx, src, axis=0):
    return tgt.at[idx].add(src)

def _segment_sum(src, seg, n):
    return jax.ops.segment_sum(src, seg, n)
kernel_name = 'mk_adaln_d1_jaxref_r8_7af9f9'

def setup_inputs(seed: int=0):
    np.random.seed(seed)
    _w = jnp.asarray

    def _L0_attn_setup():
        import jax, jax.numpy as jnp
        import numpy as np
        D_MODEL = 128
        N_HEADS = 16
        D_HEAD = D_MODEL // N_HEADS
        EPS = 1e-05

        def _forward(x, ln_g, ln_b, W_qkv, b_qkv, W_gate, b_gate, W_proj, b_proj):
            B, T, D = x.shape
            H, d = (N_HEADS, D_HEAD)
            mu = jnp.mean(x, axis=-1, keepdims=True)
            var = jnp.mean((x - mu) ** 2, axis=-1, keepdims=True)
            x_norm = (x - mu) * jax.lax.rsqrt(var + EPS) * ln_g + ln_b
            qkv = x_norm @ W_qkv + b_qkv
            q, k, v = jnp.split(qkv, 3, axis=-1)
            gate = jax.nn.sigmoid(x @ W_gate + b_gate)
            gate = gate / (jnp.mean(gate, axis=-1, keepdims=True) + EPS)
            q = (q * gate).reshape(B, T, H, d)
            k = (k * gate).reshape(B, T, H, d)
            v = v.reshape(B, T, H, d)
            q = jax.nn.relu(q.astype(jnp.float32)) ** 2 + EPS
            k = jax.nn.relu(k.astype(jnp.float32)) ** 2 + EPS
            v = v.astype(jnp.float32)
            qT = jnp.transpose(q, (1, 0, 2, 3))
            kT = jnp.transpose(k, (1, 0, 2, 3))
            vT = jnp.transpose(v, (1, 0, 2, 3))

            def step(carry, inp):
                kv_s, k_s = carry
                q_t, k_t, v_t = inp
                kv_s = kv_s + k_t[..., :, None] * v_t[..., None, :]
                k_s = k_s + k_t
                num = jnp.einsum('bhd,bhdm->bhm', q_t, kv_s)
                den = jnp.einsum('bhd,bhd->bh', q_t, k_s)[..., None] + EPS
                return ((kv_s, k_s), num / den)
            init = (jnp.zeros((B, H, d, d), jnp.float32), jnp.zeros((B, H, d), jnp.float32))
            _, outT = jax.lax.scan(step, init, (qT, kT, vT))
            out = jnp.transpose(outT, (1, 0, 2, 3)).astype(x.dtype).reshape(B, T, D)
            return out @ W_proj + b_proj
        key = jax.random.key(seed)
        ks = jax.random.split(key, 7)
        B, T = (4, 256)
        s = 1.0 / np.sqrt(D_MODEL)
        return {'x': jax.random.normal(ks[0], (B, T, D_MODEL), dtype=jnp.float32), 'ln_g': jnp.ones((D_MODEL,), jnp.float32), 'ln_b': jnp.zeros((D_MODEL,), jnp.float32), 'W_qkv': jax.random.normal(ks[1], (D_MODEL, 3 * D_MODEL), jnp.float32) * s, 'b_qkv': jnp.zeros((3 * D_MODEL,), jnp.float32), 'W_gate': jax.random.normal(ks[2], (D_MODEL, D_MODEL), jnp.float32) * s, 'b_gate': jnp.zeros((D_MODEL,), jnp.float32), 'W_proj': jax.random.normal(ks[3], (D_MODEL, D_MODEL), jnp.float32) * s, 'b_proj': jnp.zeros((D_MODEL,), jnp.float32)}
    _L0_attn_in = _L0_attn_setup()

    def _L0_ffn_setup():
        import jax, jax.numpy as jnp
        import numpy as np
        TOP_K = 2
        key = jax.random.key(seed)
        k1, k2, k3, k4 = jax.random.split(key, 4)
        B, T, D, H, E = (2, 256, 128, 256, 8)
        x = jax.random.normal(k1, (B, T, D), dtype=jnp.float32)
        w12 = jax.random.normal(k2, (E, 2 * H, D), dtype=jnp.float32) * D ** (-0.5)
        w3 = jax.random.normal(k3, (E, D, H), dtype=jnp.float32) * H ** (-0.5)
        gate_w = jax.random.normal(k4, (E, D), dtype=jnp.float32) * D ** (-0.5)
        return {'x': x, 'w12': w12, 'w3': w3, 'gate_w': gate_w}
    _L0_ffn_in = _L0_ffn_setup()
    _L0_c = _w((lambda *s: np.random.randn(*s).astype(np.float32) * 0.05)(8, 128))
    _L0_wmod = _w((lambda *s: np.random.randn(*s).astype(np.float32) * 0.05)(128, 6 * 128) * 128 ** (-0.5))
    _d = {'L0_attn_x': _L0_attn_in['x'], 'L0_attn_ln_g': _L0_attn_in['ln_g'], 'L0_attn_ln_b': _L0_attn_in['ln_b'], 'L0_attn_W_qkv': _L0_attn_in['W_qkv'], 'L0_attn_b_qkv': _L0_attn_in['b_qkv'], 'L0_attn_W_gate': _L0_attn_in['W_gate'], 'L0_attn_b_gate': _L0_attn_in['b_gate'], 'L0_attn_W_proj': _L0_attn_in['W_proj'], 'L0_attn_b_proj': _L0_attn_in['b_proj'], 'L0_ffn_w12': _L0_ffn_in['w12'], 'L0_ffn_w3': _L0_ffn_in['w3'], 'L0_ffn_gate_w': _L0_ffn_in['gate_w'], 'L0_c': _L0_c, 'L0_wmod': _L0_wmod}
    _x0 = _d['L0_attn_x']
    _d['L0_attn_x'] = jax.random.normal(jax.random.fold_in(jax.random.key(seed), 1), (8, 512, 128), dtype=_x0.dtype)
    del _x0
    return _d

def reference(L0_attn_x, L0_attn_ln_g, L0_attn_ln_b, L0_attn_W_qkv, L0_attn_b_qkv, L0_attn_W_gate, L0_attn_b_gate, L0_attn_W_proj, L0_attn_b_proj, L0_ffn_w12, L0_ffn_w3, L0_ffn_gate_w, L0_c, L0_wmod):

    def _L0_attn_ref(x, ln_g, ln_b, W_qkv, b_qkv, W_gate, b_gate, W_proj, b_proj):
        import jax, jax.numpy as jnp
        import numpy as np
        D_MODEL = 128
        N_HEADS = 16
        D_HEAD = D_MODEL // N_HEADS
        EPS = 1e-05

        def _forward(x, ln_g, ln_b, W_qkv, b_qkv, W_gate, b_gate, W_proj, b_proj):
            B, T, D = x.shape
            H, d = (N_HEADS, D_HEAD)
            mu = jnp.mean(x, axis=-1, keepdims=True)
            var = jnp.mean((x - mu) ** 2, axis=-1, keepdims=True)
            x_norm = (x - mu) * jax.lax.rsqrt(var + EPS) * ln_g + ln_b
            qkv = x_norm @ W_qkv + b_qkv
            q, k, v = jnp.split(qkv, 3, axis=-1)
            gate = jax.nn.sigmoid(x @ W_gate + b_gate)
            gate = gate / (jnp.mean(gate, axis=-1, keepdims=True) + EPS)
            q = (q * gate).reshape(B, T, H, d)
            k = (k * gate).reshape(B, T, H, d)
            v = v.reshape(B, T, H, d)
            q = jax.nn.relu(q.astype(jnp.float32)) ** 2 + EPS
            k = jax.nn.relu(k.astype(jnp.float32)) ** 2 + EPS
            v = v.astype(jnp.float32)
            qT = jnp.transpose(q, (1, 0, 2, 3))
            kT = jnp.transpose(k, (1, 0, 2, 3))
            vT = jnp.transpose(v, (1, 0, 2, 3))

            def step(carry, inp):
                kv_s, k_s = carry
                q_t, k_t, v_t = inp
                kv_s = kv_s + k_t[..., :, None] * v_t[..., None, :]
                k_s = k_s + k_t
                num = jnp.einsum('bhd,bhdm->bhm', q_t, kv_s)
                den = jnp.einsum('bhd,bhd->bh', q_t, k_s)[..., None] + EPS
                return ((kv_s, k_s), num / den)
            init = (jnp.zeros((B, H, d, d), jnp.float32), jnp.zeros((B, H, d), jnp.float32))
            _, outT = jax.lax.scan(step, init, (qT, kT, vT))
            out = jnp.transpose(outT, (1, 0, 2, 3)).astype(x.dtype).reshape(B, T, D)
            return out @ W_proj + b_proj
        return _forward(x, ln_g, ln_b, W_qkv, b_qkv, W_gate, b_gate, W_proj, b_proj)

    def _L0_ffn_ref(x, w12, w3, gate_w):
        import jax, jax.numpy as jnp
        import numpy as np
        TOP_K = 2
        E = gate_w.shape[0]
        H = w3.shape[-1]
        scores = jnp.einsum('btd,ed->bte', x, gate_w)
        topk_scores, topk_idx = jax.lax.top_k(scores, TOP_K)
        topk_probs = jax.nn.softmax(topk_scores, axis=-1)
        total_probs = jnp.sum(jax.nn.one_hot(topk_idx, E, dtype=topk_probs.dtype) * topk_probs[..., None], axis=-2)
        h12 = jnp.einsum('btd,ehd->bteh', x, w12)
        h1, h2 = (h12[..., :H], h12[..., H:])
        hidden = jax.nn.silu(h1) * h2
        expert_out = jnp.einsum('bteh,edh->bted', hidden, w3)
        y = jnp.sum(total_probs[..., None] * expert_out, axis=-2)
        return y
    x = L0_attn_x
    mod = (_silu(L0_c) @ L0_wmod).reshape(L0_c.shape[0], 6, 1, -1)
    sa, ca, ga, sb, cb, gb = (mod[:, 0], mod[:, 1], mod[:, 2], mod[:, 3], mod[:, 4], mod[:, 5])
    ga = (2 * (ga >= 0) - 1) * jnp.maximum(jnp.abs(ga), 0.25)
    gb = (2 * (gb >= 0) - 1) * jnp.maximum(jnp.abs(gb), 0.25)
    h = _layernorm(x, axis=-1) * (1 + ca) + sa
    x = x + ga * _L0_attn_ref(h, L0_attn_ln_g, L0_attn_ln_b, L0_attn_W_qkv, L0_attn_b_qkv, L0_attn_W_gate, L0_attn_b_gate, L0_attn_W_proj, L0_attn_b_proj)
    h = _layernorm(x, axis=-1) * (1 + cb) + sb
    x = x + gb * _L0_ffn_ref(h, L0_ffn_w12, L0_ffn_w3, L0_ffn_gate_w)
    return x

_drawn_inputs = setup_inputs


def setup_inputs(seed=0):
    import zlib

    import numpy as np

    out = dict(_drawn_inputs(seed))
    spreads = {'L0_attn_ln_g': (1.0, 0.2),
     'L0_attn_ln_b': (0.0, 0.1),
     'L0_attn_b_qkv': (0.0, 0.1),
     'L0_attn_b_gate': (0.0, 0.8),
     'L0_attn_b_proj': (0.0, 0.279)}
    factors = {}
    for name, (base, spread) in spreads.items():
        noise = np.random.default_rng([zlib.crc32(name.encode()), seed]).standard_normal(out[name].shape)
        drawn = base * np.exp(spread * noise) if base else spread * noise
        out[name] = jnp.asarray(drawn.astype(out[name].dtype))
    for name, factor in factors.items():
        out[name] = (out[name] * factor).astype(out[name].dtype)
    return out
```

```python
import concourse.bass as bass
from concourse import mybir
from contextlib import ExitStack


def adaln_block(nc, x, ln_g, ln_b, w_qkv, b_qkv, w_gate, b_gate, w_proj, b_proj, w12, w3, gate_w, c, wmod, out):
    fp32 = mybir.dt.float32
    f32r = mybir.dt.float32r
    ALU = mybir.AluOpType
    ACT = mybir.ActivationFunctionType
    AX = mybir.AxisListType

    B, T, D = x.shape
    NT = T // 128
    HEADS, DH = 16, D // 16
    E, H2, _ = w12.shape
    H = H2 // 2
    KH = H // 128
    EPS = 1e-5
    LN_EXP_SET = 6
    G_, LB_, BQ_, BK_, BV_, BG_, BP_, C_, GW_ = 0, 1, 2, 3, 4, 5, 6, 7, 7 + B
    NROWS = 7 + B + E
    SA, CA, GA, SB, CB, GB = range(6)

    ctx = ExitStack()
    with ctx:
        def sb(name, shape, dt=fp32):
            return ctx.enter_context(nc.sbuf_tensor(name, shape, dt))

        def sem(name):
            return ctx.enter_context(nc.semaphore(name))

        def two(name, shape, dt=fp32):
            return [sb(f"{name}{n}", shape, dt) for n in range(2)]

        x_all = sb("x_all", [128, B * NT, D])
        hc_all = sb("hc_all", [128, B * T])
        sg_all = sb("sg_all", [128, B * T])
        h2hi_all = sb("h2hi_all", [128, B * T], f32r)
        h2lo_all = sb("h2lo_all", [128, B * T], f32r)
        acc_all = sg_all[:, :].rearrange("p (n d) -> p n d", d=D)
        score_all = sb("score_all", [128, B * NT, E])
        prob_all = sb("prob_all", [128, B * NT, E])

        ident = sb("ident", [128, 128])
        centre = sb("centre", [128, 128])
        mean_w = sb("mean_w", [128, 128])
        headsum = sb("headsum", [128, 128])
        sel = sb("sel", [128, DH, 128])
        sel_r = sb("sel_r", [128, DH, 128], f32r)
        proj_j = sb("proj_j", [128, DH, 128])
        minus_half = sb("minus_half", [128, NT])
        eps_tiles = sb("eps_tiles", [128, NT])
        spare = sb("spare", [128, 1])
        eps_col = sb("eps_col", [128, 1])
        rows = sb("rows", [NROWS, D])
        cols = sb("cols", [128, NROWS])
        silu_c = sb("silu_c", [128, B])
        wmod_sb = sb("wmod_sb", [128, 6 * D])
        wqkv_sb = sb("wqkv_sb", [128, 3 * D])
        wqkv_g = sb("wqkv_g", [128, 3 * D])
        wgate_sb = sb("wgate_sb", [128, D])
        wproj_sb = sb("wproj_sb", [128, D])
        bias_qkv = sb("bias_qkv", [128, 3])
        mod = sb("mod", [128, 6, B])
        ga_sign = sb("ga_sign", [128, B])
        ga_abs = sb("ga_abs", [128, B])
        ga = sb("ga", [128, B])
        ga_bp = sb("ga_bp", [128, B])
        gb_raw, gb_sign, silu_cb = [hc_all[:, n * B * D:(n + 1) * B * D].rearrange("p (b d) -> p b d", d=D)
                                    for n in range(3)]
        gb_row = sb("gb_row", [128, B, D])

        stats = two("stats", [128, NT, 6])
        meanvar = two("meanvar", [128, NT, 2])
        vareps = two("vareps", [128, NT])
        rstd = two("rstd", [128, NT])
        xn = two("xn", [128, NT, D])
        hT = two("hT", [128, T])

        sq = sb("sq", [128, T])
        ln_var = sb("ln_var", [128, T])
        rstd2 = sb("rstd2", [128, T])
        ln_gm = sb("ln_gm", [128, T])
        inv_gm = sb("inv_gm", [128, T])
        xh = sb("xh", [128, T])
        gate = sb("gate", [128, T])
        tk = sb("tk", [128, T])
        uk = sb("uk", [128, T])
        kT = two("kT", [128, T])
        tq = sb("tq", [128, T])
        uq = sb("uq", [128, T])
        qT = two("qT", [128, T])
        v_hi = two("v_hi", [128, T], f32r)
        v_lo = two("v_lo", [128, T], f32r)
        ksum = sb("ksum", [128, T])
        qk = sb("qk", [128, T])
        ln_den = sb("ln_den", [128, T])
        inv_den = sb("inv_den", [128, T])
        qn = two("qn", [128, T])
        kv = two("kv", [128, T])
        kvsum = two("kvsum", [128, T])
        NW = 4
        qkv_j = [sb(f"qkv_j{n}", [128, T]) for n in range(NW)]
        yT = sb("yT", [128, T])

        iota_i = sb("iota_i", [128, E], mybir.dt.int32)
        iota_e = sb("iota_e", [128, E])
        rt = [sb(f"rt{n}", [128, B * NT, E]) for n in range(3)]
        hot1 = sb("hot1", [128, B * NT, E])
        top = [sb(f"top{n}", [128, B * NT]) for n in range(6)]

        w12_nat = two("w12_nat", [128, H2 // 128, D])
        w3_nat = two("w3_nat", [128, H])
        w12_hi = two("w12_hi", [128, H2], f32r)
        w12_lo = two("w12_lo", [128, H2], f32r)
        w3T = two("w3T", [128, H])
        act_h = [[tk, uk], kT]
        hid = [[tq, uq], qT]

        bank = [ctx.enter_context(nc.psum_tensor(f"bank{n}", [128, 512], fp32)) for n in range(8)]

        names = """x_first x_rest small_in wqkv_in wgate_in wproj_in wmod_in bpr_in gb_raw_ready
            ident0 ident_ready consts selects cols_p cols_ready siluc silucb modp gbp gbraw setup_v biasp projp projj wsetup
            stats_done meanvar_done vareps_done rstd_done xn_done xnT_done hT_done hc_p z_p hc_done sg_done
            sq_done var_p lnvar_done rstd2_done gm_p lngm_done invgm_done xh_done gate_done k_p v_p q_p
            tk_done uk_done k_done tq_done uq_done q_done vhi_done vlo_done ksum_done qk_done den_p lnden_done
            invden_done qn_done vrep_p kv_done kvsum_done qkvj_done y_p yT_done x2T_p x2_done
            cstats_done cmeanvar_done cvareps_done crstd_done cxn_done cxnT_done h2T_done h2hi_done h2lo_done
            score_p score_done route prob_done acc_zero out_scaled exp_done
            w12_in0 w12_in1 w3_in0 w3_in1 w12T_p w3T_p w12hi_done w12lo_done w3T_done
            up_p silu_done hid_done down_p acc_done res_done stored""".split()
        s = {n: sem("s_" + n) for n in names}

        block = ctx.enter_context(nc.Block())

        PRIMED = {"xnT_done", "cxnT_done", "x2T_p", "score_p", "hc_done", "sg_done", "x2_done", "h2lo_done",
                  "h2T_done", "score_done"}

        def prime(eng, *names):
            for name in names:
                eng.sem_inc(s[name], 1)

        def wait(eng, name, count):
            if isinstance(count, int) and count <= 0:
                return
            eng.wait_ge(s[name], count + 1 if name in PRIMED else count)

        def pipelined(eng, step):
            step(-1, 1, False, True, False)
            step(0, 0, True, True, False)
            with eng.Fori(1, B - 2, 2) as b:
                step(b, 1, True, True, True)
                step(b + 1, 0, True, True, True)
            step(B - 1, 1, True, False, True)
            step(B, 0, False, False, True)

        def experts(eng, prepare, step):
            def batches(e, q, before):
                step(e, 0, q, 0, before)
                step(e, 1, q, 1, (e, 0, q, 0))
                with eng.Fori(2, B - 1, 2) as b:
                    step(e, b, q, 0, (e, b - 1, q, 1))
                    step(e, b + 1, q, 1, (e, b, q, 0))

            prepare(0, 0)
            prepare(1, 1)
            batches(0, 0, None)
            with eng.Fori(1, E - 2, 2) as e:
                prepare(e + 1, 0)
                batches(e, 1, (e - 1, B - 1, 0, 1))
                prepare(e + 2, 1)
                batches(e + 1, 0, (e, B - 1, 1, 1))
            batches(E - 1, 1, (E - 2, B - 1, 0, 1))

        def batch(buf, b):
            return buf[:, bass.ds(b * T, T)]

        def tiles(buf, b):
            return buf[:, bass.ds(b * NT, NT), :]

        def column(buf2d, b):
            return buf2d[:, bass.ds(b, 1)]

        @block.sync
        def _(sp):
            x_t = x.rearrange("b (n p) d -> p (b n) d", p=128)
            out_t = out.rearrange("b (n p) d -> p (b n) d", p=128)
            sp.dma_start(x_all[:, 0:2 * NT, :], x_t[:, 0:2 * NT, :]).then_inc(s["x_first"], 16)
            sp.dma_start(wmod_sb[:, :], wmod).then_inc(s["wmod_in"], 16)
            sp.dma_start(wqkv_sb[:, :], w_qkv).then_inc(s["wqkv_in"], 16)
            sp.dma_start(wgate_sb[:, :], w_gate).then_inc(s["wgate_in"], 16)
            sp.dma_start(wproj_sb[:, :], w_proj).then_inc(s["wproj_in"], 16)
            sp.dma_start(x_all[:, 2 * NT:, :], x_t[:, 2 * NT:, :]).then_inc(s["x_rest"], 16)

            def load_expert(e, q):
                wait(sp, "w12T_p", e - 1)
                wait(sp, "w3T_p", e - 1)
                sp.dma_start(w12_nat[q][:, :, :], w12[bass.ds(e, 1)].rearrange("e (a p) d -> p (e a) d", p=128))\
                    .then_inc(s[f"w12_in{q}"], 16)
                sp.dma_start(w3_nat[q][:, :], w3[bass.ds(e, 1)].rearrange("e d h -> d (e h)"))\
                    .then_inc(s[f"w3_in{q}"], 16)

            load_expert(0, 0)
            load_expert(1, 1)
            with sp.Fori(2, E - 1, 2) as e:
                load_expert(e, 0)
                load_expert(e + 1, 1)

            with sp.Fori(0, B) as b:
                sp.wait_ge(s["res_done"], b + 1)
                sp.dma_start(out_t[:, bass.ds(b * NT, NT), :], tiles(acc_all, b)).then_inc(s["stored"], 16)
            sp.wait_ge(s["stored"], 16 * B)

        @block.gpsimd
        def _(pool):
            pool.memset(ident[:, :], 0.0).then_inc(s["ident0"], 1)
            pool.memset(sel[:, :, :], 0.0).then_inc(s["ident0"], 1)
            pool.memset(headsum[:, :], 1.0).then_inc(s["ident0"], 1)
            pool.wait_ge(s["ident0"], 3)
            pool.affine_select(out=ident[:, :], in_=ident[:, :], compare_op=ALU.not_equal, fill=1.0, base=0,
                               pattern=[[-1, 128]], channel_multiplier=1).then_inc(s["ident_ready"], 1)
            pool.memset(minus_half[:, :], -0.5).then_inc(s["consts"], 1)
            pool.memset(eps_tiles[:, :], EPS).then_inc(s["consts"], 1)
            pool.memset(mean_w[:, :], 1.0 / D).then_inc(s["consts"], 1)
            pool.affine_select(out=sel[:, :, :].rearrange("p j (h i) -> p j h i", i=DH),
                               in_=sel[:, :, :].rearrange("p j (h i) -> p j h i", i=DH),
                               compare_op=ALU.not_equal, fill=1.0, base=0,
                               pattern=[[-1, DH], [-DH, HEADS], [0, DH]], channel_multiplier=1)\
                .then_inc(s["selects"], 1)
            hs = headsum[:, :].rearrange("p (h i) -> p h i", i=DH)
            pool.affine_select(out=hs, in_=hs, compare_op=ALU.is_ge, fill=0.0, base=0,
                               pattern=[[-DH, HEADS], [0, DH]], channel_multiplier=1).then_inc(s["selects"], 1)
            pool.wait_ge(s["selects"], 2)
            pool.affine_select(out=hs, in_=hs, compare_op=ALU.is_ge, fill=0.0, base=DH - 1,
                               pattern=[[DH, HEADS], [0, DH]], channel_multiplier=-1).then_inc(s["selects"], 1)
            pool.iota(iota_i[:, :], pattern=[[1, E]], base=0, channel_multiplier=0).then_inc(s["selects"], 1)

            def rstd_of(prefix, f, p):
                wait(pool, f"{prefix}meanvar_done", f + 1)
                wait(pool, f"{prefix}xn_done", f - 1)
                pool.tensor_tensor(vareps[p][:, :], meanvar[p][:, :, 1], eps_tiles[:, :], ALU.add)\
                    .then_inc(s[f"{prefix}vareps_done"], 1)
                wait(pool, f"{prefix}vareps_done", f + 1)
                pool.tensor_tensor(rstd[p][:, :], vareps[p][:, :], minus_half[:, :], ALU.pow)\
                    .then_inc(s[f"{prefix}rstd_done"], 1)

            def step_ac(prefix):
                def step(b, p, has_back, has_front, has_old):
                    if has_front:
                        rstd_of(prefix, b + 1, 1 - p)
                return step

            pool.wait_ge(s["consts"], 3)
            pipelined(pool, step_ac(""))

            def step_b(b, p, has_back, has_front, has_old):
                f, fp = b + 1, 1 - p
                for j in range(DH):
                    if j == 1 and has_front:
                        wait(pool, "rstd2_done", f + 1)
                        wait(pool, "q_p", f)
                        pool.tensor_tensor(xh[:, :], batch(hc_all, f), rstd2[:, :], ALU.mult)\
                            .then_inc(s["xh_done"], 1)
                        wait(pool, "invgm_done", f + 1)
                        wait(pool, "tq_done", f)
                        pool.tensor_tensor(gate[:, :], batch(sg_all, f), inv_gm[:, :], ALU.mult)\
                            .then_inc(s["gate_done"], 1)
                    if has_back:
                        wait(pool, "kvsum_done", b * DH + (j + 1))
                        wait(pool, "y_p", b * DH + (j + 1 - NW))
                        wait(pool, "qn_done", b + 1)
                        pool.tensor_tensor(qkv_j[j % NW][:, :], kvsum[j % 2][:, :], qn[p][:, :], ALU.mult)\
                            .then_inc(s["qkvj_done"], 1)
                    if j == 5 and has_front:
                        wait(pool, "ksum_done", f + 1)
                        wait(pool, "q_done", f + 1)
                        wait(pool, "den_p", f)
                        pool.tensor_tensor(qk[:, :], ksum[:, :], qT[fp][:, :], ALU.mult).then_inc(s["qk_done"], 1)
                    if j == 7 and has_front:
                        wait(pool, "invden_done", f + 1)
                        pool.tensor_tensor(qn[fp][:, :], qT[fp][:, :], inv_den[:, :], ALU.mult)\
                            .then_inc(s["qn_done"], 1)

            pipelined(pool, step_b)
            pool.wait_ge(s["gate_done"], B)
            pool.memset(acc_all, 0.0).then_inc(s["acc_zero"], 1)
            pipelined(pool, step_ac("c"))

        @block.scalar
        def _(act):
            prime(act, "hc_done", "sg_done", "h2T_done")
            act.dma_start(rows[G_:G_ + 1, :], ln_g.rearrange("(a d) -> a d", a=1)).then_inc(s["small_in"], 16)
            act.dma_start(rows[LB_:LB_ + 1, :], ln_b.rearrange("(a d) -> a d", a=1)).then_inc(s["small_in"], 16)
            act.dma_start(rows[BQ_:BQ_ + 3, :], b_qkv.rearrange("(a d) -> a d", a=3)).then_inc(s["small_in"], 16)
            act.dma_start(rows[BG_:BG_ + 1, :], b_gate.rearrange("(a d) -> a d", a=1)).then_inc(s["small_in"], 16)
            act.dma_start(rows[BP_:BP_ + 1, :], b_proj.rearrange("(a d) -> a d", a=1)).then_inc(s["small_in"], 16)
            act.dma_start(rows[C_:C_ + B, :], c).then_inc(s["small_in"], 16)
            act.dma_start(rows[GW_:GW_ + E, :], gate_w).then_inc(s["small_in"], 16)

            act.wait_ge(s["cols_ready"], 1)
            act.activation(silu_c[:, :], cols[:, C_:C_ + B], ACT.Silu).then_inc(s["siluc"], 1)
            act.wait_ge(s["gbp"], 1)
            act.activation(gb_raw[:, 0:B // 2, :], bank[2][:, :].rearrange("p (b d) -> p b d", d=D), ACT.Copy)\
                .then_inc(s["gbraw"], 1)
            act.activation(gb_raw[:, B // 2:B, :], bank[3][:, :].rearrange("p (b d) -> p b d", d=D), ACT.Copy)\
                .then_inc(s["gbraw"], 1)
            act.wait_ge(s["projp"], 1)
            act.activation(proj_j[:, 0:DH // 2, :], bank[5][:, :].rearrange("p (b d) -> p b d", d=D), ACT.Copy)
            act.activation(proj_j[:, DH // 2:DH, :], bank[6][:, :].rearrange("p (b d) -> p b d", d=D), ACT.Copy)\
                .then_inc(s["projj"], 1)
            act.wait_ge(s["setup_v"], 1)

            def step_a(b, p, has_back, has_front, has_old):
                if has_front:
                    f, fp = b + 1, 1 - p
                    wait(act, "xnT_done", f + 1)
                    wait(act, "z_p", f - 1)
                    act.activation(hT[fp][:, :], bank[fp][:, :], ACT.Identity, bias=column(mod[:, SA, :], f),
                                   scale=column(mod[:, CA, :], f)).then_inc(s["hT_done"], 1)
                if has_back:
                    wait(act, "hc_p", b + 1)
                    act.activation(batch(hc_all, b), bank[2 + p][:, :], ACT.Copy).then_inc(s["hc_done"], 1)
                    wait(act, "z_p", b + 1)
                    act.activation(batch(sg_all, b), bank[4 + p][:, :], ACT.Sigmoid, bias=cols[:, BG_:BG_ + 1])\
                        .then_inc(s["sg_done"], 1)

            pipelined(act, step_a)

            act.add_instruction(mybir.InstLoadActFuncSet(name=nc.get_next_instruction_name(), act_func_set_id=LN_EXP_SET,
                                                         engine=mybir.EngineType.Activation))

            def step_b(b, p, has_back, has_front, has_old):
                f, fp = b + 1, 1 - p
                if has_front:
                    wait(act, "hc_done", B)
                    wait(act, "var_p", f)
                    act.activation(sq[:, :], batch(hc_all, f), ACT.Square).then_inc(s["sq_done"], 1)
                    wait(act, "var_p", f + 1)
                    act.activation(ln_var[:, :], bank[0][:, :], ACT.Ln, bias=eps_col[:, :]).then_inc(s["lnvar_done"], 1)
                    wait(act, "lnvar_done", f + 1)
                    wait(act, "xh_done", f)
                    act.activation(rstd2[:, :], ln_var[:, :], ACT.Exp, scale=-0.5).then_inc(s["rstd2_done"], 1)
                    wait(act, "gm_p", f + 1)
                    act.activation(ln_gm[:, :], bank[1][:, :], ACT.Ln, bias=eps_col[:, :]).then_inc(s["lngm_done"], 1)
                    wait(act, "lngm_done", f + 1)
                    wait(act, "gate_done", f)
                    act.activation(inv_gm[:, :], ln_gm[:, :], ACT.Exp, scale=-1.0).then_inc(s["invgm_done"], 1)
                if has_old:
                    wait(act, "y_p", b * DH)
                    wait(act, "x2T_p", b - 1)
                    act.activation(yT[:, :], bank[7][:, :], ACT.Identity, bias=column(ga_bp, b - 1),
                                   scale=column(ga, b - 1)).then_inc(s["yT_done"], 1)
                if has_front:
                    wait(act, "v_p", f + 1)
                    wait(act, "vrep_p", f * DH - DH)
                    act.activation(v_hi[fp][:, :], bank[4][:, :], ACT.Identity, bias=bias_qkv[:, 2:3])\
                        .then_inc(s["vhi_done"], 1)
                    wait(act, "den_p", f + 1)
                    act.activation(ln_den[:, :], bank[0][:, :], ACT.Ln, bias=eps_col[:, :]).then_inc(s["lnden_done"], 1)
                    wait(act, "lnden_done", f + 1)
                    wait(act, "qn_done", f)
                    act.activation(inv_den[:, :], ln_den[:, :], ACT.Exp, scale=-1.0).then_inc(s["invden_done"], 1)

            pipelined(act, step_b)

            def step_c(b, p, has_back, has_front, has_old):
                if has_back:
                    wait(act, "cxnT_done", b + 1)
                    wait(act, "h2lo_done", b - 1)
                    wait(act, "score_p", b - 1)
                    act.activation(hT[p][:, :], bank[p][:, :], ACT.Identity, bias=column(mod[:, SB, :], b),
                                   scale=column(mod[:, CB, :], b)).then_inc(s["h2T_done"], 1)
                    wait(act, "h2T_done", b + 1)
                    act.activation(batch(h2hi_all, b), hT[p][:, :], ACT.Copy).then_inc(s["h2hi_done"], 1)

            pipelined(act, step_c)
            act.wait_ge(s["prob_done"], 1)
            act.activation(top[4][:, :], top[4][:, :], ACT.Exp).then_inc(s["exp_done"], 1)

            def prepare(e, q):
                wait(act, "w12T_p", e + 1)
                wait(act, "down_p", (e - 1) * B)
                act.activation(w12_hi[q][:, :], bank[6][:, :], ACT.Copy).then_inc(s["w12hi_done"], 1)
                wait(act, "w3T_p", e + 1)
                act.activation(w3T[q][:, :], bank[7][:, 0:H], ACT.Copy).then_inc(s["w3T_done"], 1)

            def step_d(e, b, q, p, before):
                n = e * B + b
                for k in range(KH):
                    wait(act, "up_p", n * KH + (k + 1))
                    wait(act, "hid_done", n * KH + (k + 1 - 2 * KH))
                    act.activation(act_h[k][p][:, :], bank[2 * k][:, :], ACT.Silu).then_inc(s["silu_done"], 1)

            experts(act, prepare, step_d)

        @block.vector
        def _(dve):
            prime(dve, "x2_done", "h2lo_done", "score_done")
            dve.memset(eps_col[:, :], EPS).then_inc(s["wsetup"], 1)
            dve.wait_ge(s["cols_p"], 1)
            dve.tensor_copy(cols[:, :], bank[0][:, 0:NROWS]).then_inc(s["cols_ready"], 1)
            dve.wait_ge(s["ident_ready"], 1)
            dve.tensor_scalar(centre[:, :], ident[:, :], -1.0 / D, 1.0, ALU.add, ALU.mult).then_inc(s["wsetup"], 1)
            dve.wait_ge(s["wqkv_in"], 16)
            dve.wait_ge(s["cols_ready"], 1)
            dve.tensor_scalar(wqkv_g[:, :], wqkv_sb[:, :], cols[:, G_:G_ + 1], None, ALU.mult).then_inc(s["wsetup"], 1)
            dve.wait_ge(s["selects"], 4)
            dve.tensor_copy(sel_r[:, :, :], sel[:, :, :]).then_inc(s["wsetup"], 1)
            dve.tensor_copy(iota_e[:, :], iota_i[:, :]).then_inc(s["wsetup"], 1)
            dve.wait_ge(s["siluc"], 1)
            dve.tensor_copy(silu_cb[:, :, :], silu_c[:, :].unsqueeze(2).to_broadcast([128, B, 128]))\
                .then_inc(s["silucb"], 1)
            dve.wait_ge(s["modp"], 1)
            dve.tensor_copy(mod[:, :, :], bank[1][:, 0:6 * B].rearrange("p (c b) -> p c b", b=B)).then_inc(s["wsetup"], 1)
            dve.wait_ge(s["wsetup"], 6)
            for ch in (CA, CB):
                dve.tensor_scalar(mod[:, ch, :], mod[:, ch, :], 1.0, None, ALU.add).then_inc(s["wsetup"], 1)
            dve.tensor_scalar(ga_sign[:, :], mod[:, GA, :], 0.0, 2.0, ALU.is_ge, ALU.mult).then_inc(s["wsetup"], 1)
            dve.wait_ge(s["wsetup"], 9)
            dve.scalar_tensor_tensor(ga_abs[:, :], ga_sign[:, :], -1.0, mod[:, GA, :], ALU.add, ALU.mult)\
                .then_inc(s["wsetup"], 1)
            dve.wait_ge(s["wsetup"], 10)
            dve.tensor_scalar(ga_abs[:, :], ga_abs[:, :], 0.25, None, ALU.max).then_inc(s["wsetup"], 1)
            dve.wait_ge(s["wsetup"], 11)
            dve.scalar_tensor_tensor(ga[:, :], ga_sign[:, :], -1.0, ga_abs[:, :], ALU.add, ALU.mult)\
                .then_inc(s["wsetup"], 1)
            dve.wait_ge(s["wsetup"], 12)
            dve.tensor_scalar(ga_bp[:, :], ga[:, :], cols[:, BP_:BP_ + 1], None, ALU.mult).then_inc(s["wsetup"], 1)
            dve.wait_ge(s["biasp"], 1)
            dve.tensor_tensor(bias_qkv[:, :], bank[4][:, 0:3], cols[:, BQ_:BQ_ + 3], ALU.add).then_inc(s["wsetup"], 1)
            dve.wait_ge(s["gbraw"], 2)
            dve.tensor_scalar(gb_sign[:, :, :], gb_raw[:, :, :], 0.0, 2.0, ALU.is_ge, ALU.mult).then_inc(s["wsetup"], 1)
            dve.wait_ge(s["wsetup"], 15)
            dve.scalar_tensor_tensor(gb_row[:, :, :], gb_sign, -1.0, gb_raw, ALU.add, ALU.mult).then_inc(s["wsetup"], 1)
            dve.wait_ge(s["wsetup"], 16)
            dve.tensor_scalar(gb_row[:, :, :], gb_row[:, :, :], 0.25, None, ALU.max).then_inc(s["wsetup"], 1)
            dve.wait_ge(s["wsetup"], 17)
            dve.scalar_tensor_tensor(gb_row[:, :, :], gb_sign[:, :, :], -1.0, gb_row[:, :, :], ALU.add, ALU.mult)\
                .then_inc(s["wsetup"], 1)
            dve.wait_ge(s["wsetup"], 18)
            dve.memset(stats[0][:, :, :], 0.0).then_inc(s["setup_v"], 1)
            dve.wait_ge(s["setup_v"], 1)

            def batch_stats(prefix, f, fp):
                for t in range(NT):
                    last = dve.bn_stats(stats[fp][:, t, :], x_all[:, bass.ds(f * NT + t, 1), :])
                last.then_inc(s[f"{prefix}stats_done"], 1)
                wait(dve, f"{prefix}stats_done", f + 1)
                wait(dve, f"{prefix}vareps_done", f - 1)
                dve.memset(spare[:, :], 0.0)
                for t in range(NT):
                    last = dve.bn_aggr(meanvar[fp][:, t, :], stats[fp][:, t, :])
                last.then_inc(s[f"{prefix}meanvar_done"], 1)

            def normalise(prefix, b, p):
                wait(dve, f"{prefix}rstd_done", b + 1)
                wait(dve, f"{prefix}xnT_done", b - 1)
                for t in range(NT):
                    last = dve.tensor_scalar(xn[p][:, t, :], x_all[:, bass.ds(b * NT + t, 1), :],
                                             meanvar[p][:, t, 0:1], rstd[p][:, t:t + 1], ALU.subtract, ALU.mult)
                last.then_inc(s[f"{prefix}xn_done"], 1)

            def step_a(b, p, has_back, has_front, has_old):
                if has_front:
                    if isinstance(b, int):
                        dve.wait_ge(s["x_first"], 16)
                        if b == 0:
                            pass
                    else:
                        dve.wait_ge(s["x_rest"], 16)
                    batch_stats("", b + 1, 1 - p)
                if has_back:
                    normalise("", b, p)

            pipelined(dve, step_a)

            def step_b(b, p, has_back, has_front, has_old):
                f, fp = b + 1, 1 - p
                for j in range(DH):
                    if has_back:
                        wait(dve, "vrep_p", b * DH + (j + 1))
                        dve.tensor_tensor(kv[j % 2][:, :], bank[5 + j % 2][:, :], kT[p][:, :], ALU.mult)\
                            .then_inc(s["kv_done"], 1)
                        wait(dve, "kv_done", b * DH + (j + 1))
                        wait(dve, "qkvj_done", b * DH + (j + 1 - 2))
                        dve.tensor_tensor_scan(kvsum[j % 2][:, :], kv[j % 2][:, :], kv[j % 2][:, :], 0.0,
                                               ALU.add, ALU.bypass).then_inc(s["kvsum_done"], 1)
                    if j == 3 and has_front:
                        wait(dve, "k_p", f + 1)
                        wait(dve, "gate_done", f + 1)
                        dve.scalar_tensor_tensor(tk[:, :], bank[3][:, :], bias_qkv[:, 1:2], gate[:, :],
                                                 ALU.add, ALU.mult).then_inc(s["tk_done"], 1)
                        wait(dve, "tk_done", f + 1)
                        dve.scalar_tensor_tensor(uk[:, :], tk[:, :], 0.0, tk[:, :], ALU.max, ALU.mult)\
                            .then_inc(s["uk_done"], 1)
                        wait(dve, "uk_done", f + 1)
                        dve.tensor_scalar(kT[fp][:, :], uk[:, :], EPS, None, ALU.add).then_inc(s["k_done"], 1)
                    if j == 4:
                        if has_front:
                            wait(dve, "vhi_done", f + 1)
                            dve.scalar_tensor_tensor(v_lo[fp][:, :], bank[4][:, :], bias_qkv[:, 2:3],
                                                     v_hi[fp][:, :].bitcast(fp32), ALU.add, ALU.subtract)\
                                .then_inc(s["vlo_done"], 1)
                            wait(dve, "k_done", f + 1)
                            wait(dve, "qk_done", f)
                            dve.tensor_tensor_scan(ksum[:, :], kT[fp][:, :], kT[fp][:, :], 0.0, ALU.add, ALU.bypass)\
                                .then_inc(s["ksum_done"], 1)
                        if has_old:
                            wait(dve, "x2T_p", b)
                            dve.tensor_tensor(tiles(x_all, b - 1), bank[1][:, :].rearrange("p (n d) -> p n d", d=D),
                                              tiles(x_all, b - 1), ALU.add).then_inc(s["x2_done"], 1)
                    if j == 5 and has_front:
                        wait(dve, "q_p", f + 1)
                        dve.scalar_tensor_tensor(tq[:, :], bank[2][:, :], bias_qkv[:, 0:1], gate[:, :],
                                                 ALU.add, ALU.mult).then_inc(s["tq_done"], 1)
                        wait(dve, "tq_done", f + 1)
                        dve.scalar_tensor_tensor(uq[:, :], tq[:, :], 0.0, tq[:, :], ALU.max, ALU.mult)\
                            .then_inc(s["uq_done"], 1)
                        wait(dve, "uq_done", f + 1)
                        wait(dve, "qn_done", f - 1)
                        dve.tensor_scalar(qT[fp][:, :], uq[:, :], EPS, None, ALU.add).then_inc(s["q_done"], 1)

            pipelined(dve, step_b)

            wait(dve, "x2_done", B)

            def step_c(b, p, has_back, has_front, has_old):
                if has_front:
                    batch_stats("c", b + 1, 1 - p)
                if has_back:
                    normalise("c", b, p)
                if has_old:
                    wait(dve, "h2hi_done", b)
                    dve.tensor_tensor(batch(h2lo_all, b - 1), hT[1 - p][:, :], batch(h2hi_all, b - 1).bitcast(fp32),
                                      ALU.subtract).then_inc(s["h2lo_done"], 1)
                    wait(dve, "score_p", b)
                    dve.tensor_copy(tiles(score_all, b - 1),
                                    bank[3 - p][:, 0:NT * E].rearrange("p (n e) -> p n e", e=E))\
                        .then_inc(s["score_done"], 1)

            pipelined(dve, step_c)

            wait(dve, "score_done", B)
            chain = [0]

            def link(op):
                chain[0] += 1
                op.then_inc(s["route"], 1)
                dve.wait_ge(s["route"], chain[0])

            full = [128, B * NT, E]
            each = iota_e[:, :].unsqueeze(1).to_broadcast(full)

            def wide(t):
                return t[:, :].unsqueeze(2).to_broadcast(full)

            def first_max(scores, best, index, onehot):
                link(dve.tensor_reduce(best[:, :], scores, AX.X, ALU.max))
                link(dve.tensor_tensor(rt[0][:, :, :], scores, wide(best), ALU.is_lt))
                link(dve.scalar_tensor_tensor(rt[0][:, :, :], rt[0][:, :, :], float(E), each, ALU.mult, ALU.add))
                link(dve.tensor_reduce(index[:, :], rt[0][:, :, :], AX.X, ALU.min))
                link(dve.tensor_tensor(onehot[:, :, :], each, wide(index), ALU.is_equal))

            first_max(score_all[:, :, :], top[0], top[1], hot1)
            link(dve.scalar_tensor_tensor(rt[1][:, :, :], hot1[:, :, :], -3.0e38, score_all[:, :, :], ALU.mult, ALU.add))
            first_max(rt[1][:, :, :], top[2], top[3], rt[2])
            dve.tensor_tensor(top[4][:, :], top[2][:, :], top[0][:, :], ALU.subtract).then_inc(s["prob_done"], 1)
            dve.wait_ge(s["exp_done"], 1)
            link(dve.tensor_scalar(top[5][:, :], top[4][:, :], 1.0, None, ALU.add))
            link(dve.reciprocal(top[5][:, :], top[5][:, :]))
            link(dve.tensor_tensor(top[4][:, :], top[4][:, :], top[5][:, :], ALU.mult))
            link(dve.tensor_tensor(hot1[:, :, :], hot1[:, :, :], wide(top[5]), ALU.mult))
            link(dve.tensor_tensor(rt[2][:, :, :], rt[2][:, :, :], wide(top[4]), ALU.mult))
            link(dve.tensor_tensor(prob_all[:, :, :], hot1[:, :, :], rt[2][:, :, :], ALU.add))
            dve.wait_ge(s["acc_zero"], 1)

            def prepare(e, q):
                wait(dve, "w12hi_done", e + 1)
                dve.tensor_tensor(w12_lo[q][:, :], bank[6][:, :], w12_hi[q][:, :].bitcast(fp32), ALU.subtract)\
                    .then_inc(s["w12lo_done"], 1)

            def weigh(e, b, q, p):
                n = e * B + b
                wait(dve, "down_p", n + 1)
                if not (isinstance(e, int) and e == 0):
                    wait(dve, "acc_done", n - B + 1)
                for t in range(NT):
                    acc = acc_all[:, bass.ds(b * NT + t, 1), :]
                    last = dve.scalar_tensor_tensor(acc, bank[4 + p][:, t * D:(t + 1) * D].unsqueeze(1),
                                                    prob_all[:, bass.ds(b * NT + t, 1), bass.ds(e, 1)],
                                                    acc, ALU.mult, ALU.add)
                last.then_inc(s["acc_done"], 1)

            def step_d(e, b, q, p, before):
                n = e * B + b
                for k in range(KH):
                    wait(dve, "silu_done", n * KH + (k + 1))
                    wait(dve, "down_p", n - 1)
                    dve.tensor_tensor(hid[k][p][:, :], bank[2 * k + 1][:, :], act_h[k][p][:, :], ALU.mult)\
                        .then_inc(s["hid_done"], 1)
                if before:
                    weigh(*before)

            experts(dve, prepare, step_d)
            weigh(E - 1, B - 1, 1, 1)

            def finish(b, p):
                dve.wait_ge(s["acc_done"], (E - 1) * B + b + 1)
                dve.tensor_tensor(kv[p][:, :].rearrange("p (n d) -> p n d", d=D), tiles(acc_all, b),
                                  gb_row[:, bass.ds(b, 1), :].to_broadcast([128, NT, D]), ALU.mult)\
                    .then_inc(s["out_scaled"], 1)
                dve.wait_ge(s["out_scaled"], b + 1)
                dve.tensor_tensor(tiles(acc_all, b), kv[p][:, :].rearrange("p (n d) -> p n d", d=D),
                                  tiles(x_all, b), ALU.add).then_inc(s["res_done"], 1)

            with dve.Fori(0, B - 1, 2) as b:
                finish(b, 0)
                finish(b + 1, 1)

        @block.tensor
        def _(pe):
            prime(pe, "xnT_done", "cxnT_done", "x2T_p", "score_p")
            pe.wait_ge(s["small_in"], 16 * 7)
            pe.wait_ge(s["ident_ready"], 1)
            pe.transpose(bank[0][:, 0:NROWS], rows[:, :], ident[0:NROWS, 0:NROWS]).then_inc(s["cols_p"], 1)
            pe.wait_ge(s["siluc"], 1)
            pe.wait_ge(s["wmod_in"], 16)
            for ch in range(6):
                last = pe.matmul(bank[1][:, ch * B:(ch + 1) * B], wmod_sb[:, ch * D:(ch + 1) * D], silu_c[:, :],
                                 start=True, stop=True)
            last.then_inc(s["modp"], 1)
            pe.wait_ge(s["silucb"], 1)
            for b in range(B):
                last = pe.matmul(bank[2 + b // 4][:, b % 4 * D:(b % 4 + 1) * D], silu_cb[:, b, :],
                                 wmod_sb[:, GB * D:(GB + 1) * D], start=True, stop=True)
            last.then_inc(s["gbp"], 1)
            pe.wait_ge(s["wqkv_in"], 16)
            pe.wait_ge(s["cols_ready"], 1)
            for ch in range(3):
                last = pe.matmul(bank[4][:, ch:ch + 1], wqkv_sb[:, ch * D:(ch + 1) * D], cols[:, LB_:LB_ + 1],
                                 start=True, stop=True)
            last.then_inc(s["biasp"], 1)
            pe.wait_ge(s["selects"], 3)
            pe.wait_ge(s["wproj_in"], 16)
            for j in range(DH):
                last = pe.matmul(bank[5 + j // 4][:, j % 4 * D:(j % 4 + 1) * D], sel[:, j, :], wproj_sb[:, :],
                                 start=True, stop=True)
            last.then_inc(s["projp"], 1)
            pe.wait_ge(s["wgate_in"], 16)
            pe.wait_ge(s["setup_v"], 1)
            pe.wait_ge(s["projj"], 1)

            def transposes(prefix, b, p):
                wait(pe, f"{prefix}xn_done", b + 1)
                for t in range(NT):
                    last = pe.transpose(bank[p][:, t * 128:(t + 1) * 128], xn[p][:, t, :], ident[:, :])
                last.then_inc(s[f"{prefix}xnT_done"], 1)

            def step_a(b, p, has_back, has_front, has_old):
                if has_front:
                    wait(pe, "hT_done", b)
                    transposes("", b + 1, 1 - p)
                if has_back:
                    wait(pe, "hT_done", b + 1)
                    wait(pe, "hc_done", b - 1)
                    pe.matmul(bank[2 + p][:, :], centre[:, :], hT[p][:, :], start=True, stop=True)\
                        .then_inc(s["hc_p"], 1)
                    wait(pe, "sg_done", b - 1)
                    pe.matmul(bank[4 + p][:, :], wgate_sb[:, :], hT[p][:, :], start=True, stop=True)\
                        .then_inc(s["z_p"], 1)

            pipelined(pe, step_a)
            wait(pe, "sg_done", B)
            wait(pe, "hc_done", B)

            def v_columns(b, p, j):
                wait(pe, "vlo_done", b + 1)
                wait(pe, "kv_done", b * DH + (j + 1 - 2))
                pe.matmul(bank[5 + j % 2][:, :], sel_r[:, j, :], v_hi[p][:, :], start=True, stop=False)
                pe.matmul(bank[5 + j % 2][:, :], sel_r[:, j, :], v_lo[p][:, :], start=False, stop=True)\
                    .then_inc(s["vrep_p"], 1)

            def project(b, j):
                wait(pe, "qkvj_done", b * DH + (j + 1))
                if j == 0:
                    wait(pe, "yT_done", b)
                pe.matmul(bank[7][:, :], proj_j[:, j, :], qkv_j[j % NW][:, :], start=(j == 0), stop=(j == DH - 1))\
                    .then_inc(s["y_p"], 1)

            def step_b(b, p, has_back, has_front, has_old):
                f, fp = b + 1, 1 - p
                for j in range(DH):
                    if has_back and j + 1 < DH:
                        v_columns(b, p, j + 1)
                    if j == 0 and has_front:
                        wait(pe, "sq_done", f + 1)
                        wait(pe, "lnden_done", f)
                        pe.matmul(bank[0][:, :], mean_w[:, :], sq[:, :], start=True, stop=True)\
                            .then_inc(s["var_p"], 1)
                        wait(pe, "x2_done", b - 1)
                        pe.matmul(bank[1][:, :], mean_w[:, :], batch(sg_all, f), start=True, stop=True)\
                            .then_inc(s["gm_p"], 1)
                    if j == 2 and has_front:
                        wait(pe, "xh_done", f + 1)
                        wait(pe, "tk_done", f)
                        pe.matmul(bank[3][:, :], wqkv_g[:, D:2 * D], xh[:, :], start=True, stop=True)\
                            .then_inc(s["k_p"], 1)
                        wait(pe, "vlo_done", f)
                        pe.matmul(bank[4][:, :], wqkv_g[:, 2 * D:3 * D], xh[:, :], start=True, stop=True)\
                            .then_inc(s["v_p"], 1)
                        wait(pe, "tq_done", f)
                        pe.matmul(bank[2][:, :], wqkv_g[:, 0:D], xh[:, :], start=True, stop=True)\
                            .then_inc(s["q_p"], 1)
                    if j == 3 and has_old:
                        wait(pe, "yT_done", b)
                        wait(pe, "lngm_done", b + 2 if has_front else B)
                        for t in range(NT):
                            last = pe.transpose(bank[1][:, t * 128:(t + 1) * 128], yT[:, t * 128:(t + 1) * 128],
                                                ident[:, :])
                        last.then_inc(s["x2T_p"], 1)
                    if j >= 2 and has_back:
                        project(b, j - 2)
                    if j < 2 and has_old:
                        project(b - 1, DH - 2 + j)
                    if j == 6 and has_front:
                        wait(pe, "qk_done", f + 1)
                        wait(pe, "lnvar_done", f + 1)
                        pe.matmul(bank[0][:, :], headsum[:, :], qk[:, :], start=True, stop=True)\
                            .then_inc(s["den_p"], 1)
                if has_front:
                    v_columns(f, fp, 0)

            pipelined(pe, step_b)

            wait(pe, "lnden_done", B)
            wait(pe, "x2_done", B)
            wait(pe, "tk_done", B)
            wait(pe, "tq_done", B)

            def step_c(b, p, has_back, has_front, has_old):
                if has_back:
                    wait(pe, "h2T_done", b - 1)
                    transposes("c", b, p)
                if has_old:
                    wait(pe, "h2T_done", b)
                    wait(pe, "score_done", b - 1)
                    for t in range(NT):
                        last = pe.matmul(bank[3 - p][:, t * E:(t + 1) * E], hT[1 - p][:, t * 128:(t + 1) * 128],
                                         cols[:, GW_:GW_ + E], start=True, stop=True)
                    last.then_inc(s["score_p"], 1)

            pipelined(pe, step_c)
            wait(pe, "h2lo_done", B)
            wait(pe, "score_done", B)
            wait(pe, "kv_done", B * DH)
            wait(pe, "yT_done", B)
            wait(pe, "vlo_done", B)

            def prepare(e, q):
                wait(pe, f"w12_in{q}", 8 * (e - q) + 16)
                wait(pe, "w12lo_done", e)
                for a in range(H2 // 128):
                    last = pe.transpose(bank[6][:, a * 128:(a + 1) * 128], w12_nat[q][:, a, :], ident[:, :])
                last.then_inc(s["w12T_p"], 1)
                wait(pe, f"w3_in{q}", 8 * (e - q) + 16)
                wait(pe, "w3T_done", e)
                for k in range(KH):
                    last = pe.transpose(bank[7][:, k * 128:(k + 1) * 128], w3_nat[q][:, k * 128:(k + 1) * 128],
                                        ident[:, :])
                last.then_inc(s["w3T_p"], 1)

            def down(e, b, q, p):
                n = e * B + b
                wait(pe, "hid_done", n * KH + KH)
                wait(pe, "w3T_done", e + 1)
                wait(pe, "acc_done", n - 1)
                for t in range(NT):
                    for k in range(KH):
                        last = pe.matmul(bank[4 + p][:, t * D:(t + 1) * D], hid[k][p][:, t * 128:(t + 1) * 128],
                                         w3T[q][:, k * 128:(k + 1) * 128], start=(k == 0), stop=(k == KH - 1))
                last.then_inc(s["down_p"], 1)

            def step_d(e, b, q, p, before):
                n = e * B + b
                wait(pe, "w12lo_done", e + 1)
                for k in range(KH):
                    wait(pe, "hid_done", n * KH + (k + 1 - KH))
                    for half in range(2):
                        w = slice(half * H + k * 128, half * H + (k + 1) * 128)
                        o = bank[2 * k + half][:, :]
                        pe.matmul(o, w12_hi[q][:, w], batch(h2hi_all, b), start=True, stop=False)
                        pe.matmul(o, w12_hi[q][:, w], batch(h2lo_all, b), start=False, stop=False)
                        last = pe.matmul(o, w12_lo[q][:, w], batch(h2hi_all, b), start=False, stop=True)
                    last.then_inc(s["up_p"], 1)
                if before:
                    down(*before)

            experts(pe, prepare, step_d)
            down(E - 1, B - 1, 1, 1)


_INS = ['L0_attn_x', 'L0_attn_ln_g', 'L0_attn_ln_b', 'L0_attn_W_qkv', 'L0_attn_b_qkv', 'L0_attn_W_gate', 'L0_attn_b_gate',
        'L0_attn_W_proj', 'L0_attn_b_proj', 'L0_ffn_w12', 'L0_ffn_w3', 'L0_ffn_gate_w', 'L0_c', 'L0_wmod']
_OUTS = [((8, 512, 128), 'float32')]


def kernel(**inputs):
    import numpy as _np
    import concourse.bacc as _bacc
    from concourse import mybir as _mybir
    from concourse.bass_utils import run_bass_kernel_spmd as _run

    nc = _bacc.Bacc("TRN2", target_bir_lowering=False, num_devices=1)
    arrays, args = {}, []
    for name in _INS:
        a = _np.ascontiguousarray(inputs[name])
        if a.dtype.kind in "iu":
            a = a.astype(_np.int64)
        arrays[f"in_{name}_dram"] = a
        args.append(nc.dram_tensor(f"in_{name}_dram", a.shape, _mybir.dt.from_np(a.dtype), kind="ExternalInput").ap())
    for i, (shape, dtype) in enumerate(_OUTS):
        dt = _mybir.dt.from_np(_np.dtype(dtype))
        args.append(nc.dram_tensor(f"out_{i}_dram", shape, dt, kind="ExternalOutput").ap())
    adaln_block(nc, *args)
    r = _run(nc, [arrays], core_ids=[0])
    got = tuple(r.results[0][f"out_{i}_dram"] for i in range(len(_OUTS)))
    return got[0]
```

```python
import concourse.bass as bass
from concourse import mybir
from contextlib import ExitStack
import math


def adaln_block(nc, x, ln_g, ln_b, w_qkv, b_qkv, w_gate, b_gate, w_proj, b_proj, w12, w3, gate_w, c, wmod, out):
    fp32 = mybir.dt.float32
    f32r = mybir.dt.float32r
    ALU = mybir.AluOpType
    ACT = mybir.ActivationFunctionType
    AX = mybir.AxisListType

    B, T, D = x.shape
    NT = T // 128
    HEADS, DH = 16, D // 16
    E, H2, _ = w12.shape
    H = H2 // 2
    KH = H // 128
    EPS = 1e-5
    LN_EXP_SET = 6
    G_, LB_, BQ_, BK_, BV_, BG_, BP_, C_, GW_ = 0, 1, 2, 3, 4, 5, 6, 7, 7 + B
    NROWS = 7 + B + E
    SA, CA, GA, SB, CB, GB = range(6)
    M = E * KH
    DIFF = 11
    LINKS = 18
    FRONT_D = [[0], [1], [2, 3], [4], [5, 6], [7, 8], [9], [10, 11], [12], [13], [14], [15], [], [], [], []]
    LAG_J = 4
    LAG = 3
    RING = 4
    prob_dram = nc.dram_tensor("prob_scratch", (B, E, T), fp32).ap()

    ctx = ExitStack()
    with ctx:
        def sb(name, shape, dt=fp32):
            return ctx.enter_context(nc.sbuf_tensor(name, shape, dt))

        def sem(name):
            return ctx.enter_context(nc.semaphore(name))

        def two(name, shape, dt=fp32):
            return [sb(f"{name}{n}", shape, dt) for n in range(2)]

        x_all = sb("x_all", [128, B * NT, D])

        ident = sb("ident", [128, 128])
        centre = sb("centre", [128, 128])
        mean_w = sb("mean_w", [128, 128])
        headsum = sb("headsum", [128, 128])
        sel_r = sb("sel_r", [128, DH, 128], f32r)
        proj_j = sb("proj_j", [128, DH, 128])
        minus_half = sb("minus_half", [128, B * NT])
        eps_tiles = sb("eps_tiles", [128, B * NT])
        spare = sb("spare", [128, 1])
        eps_col = sb("eps_col", [128, 1])
        rows = sb("rows", [NROWS, D])
        cols = sb("cols", [128, NROWS])
        silu_c = sb("silu_c", [128, B])
        wmod_sb = sb("wmod_sb", [128, 6 * D])
        wqkv_sb = sb("wqkv_sb", [128, 3 * D])
        wqkv_g = sb("wqkv_g", [128, 3 * D])
        wgate_sb = sb("wgate_sb", [128, D])
        wproj_sb = sb("wproj_sb", [128, D])
        bias_qkv = sb("bias_qkv", [128, 3])
        mod = sb("mod", [128, 6, B])
        minus_bg = sb("minus_bg", [128, 1])
        g_sign = sb("g_sign", [128, 2, B])
        g_abs = sb("g_abs", [128, 2, B])
        g_ab = sb("g_ab", [128, 2, B])
        ga, gb = g_ab[:, 0, :], g_ab[:, 1, :]
        ga_bp = sb("ga_bp", [128, B])

        hc = sb("hc", [128, T])
        sg = sb("sg", [128, T])
        prob_row = sb("prob_row", [128, RING * T])
        first_stats = sb("first_stats", [128, B * NT, 6])
        first_meanvar = sb("first_meanvar", [128, B * NT, 2])
        first_vareps = sb("first_vareps", [128, B * NT])
        first_shift = sb("first_shift", [128, B * NT])
        first_rstd = sb("first_rstd", [128, B * NT])
        stats = two("stats", [128, NT, 6])
        meanvar = two("meanvar", [128, NT, 2])
        vareps = two("vareps", [128, NT])
        rstd = two("rstd", [128, NT])
        xn = two("xn", [128, NT, D])
        hT = two("hT", [128, T])

        sq = sb("sq", [128, T])
        expz = sb("expz", [128, T])
        ln_var = sb("ln_var", [128, T])
        rstd2 = sb("rstd2", [128, T])
        ln_gm = sb("ln_gm", [128, T])
        inv_gm = sb("inv_gm", [128, T])
        xh = sb("xh", [128, T])
        gate = sb("gate", [128, T])
        tk = sb("tk", [128, T])
        uk = sb("uk", [128, T])
        kT = two("kT", [128, T])
        tq = sb("tq", [128, T])
        uq = sb("uq", [128, T])
        qT = two("qT", [128, T])
        v_hi = two("v_hi", [128, T], f32r)
        v_lo = two("v_lo", [128, T], f32r)
        ksum = sb("ksum", [128, T])
        qk = sb("qk", [128, T])
        ln_den = sb("ln_den", [128, T])
        inv_den = sb("inv_den", [128, T])
        qn = two("qn", [128, T])
        kv_both = sb("kv_both", [128, 2 * T])
        kv = [kv_both[:, n * T:(n + 1) * T] for n in range(2)]
        sel = kv_both[:, :].rearrange("p (j m) -> p j m", m=128)
        kvsum = two("kvsum", [128, T])
        NW = 4
        qkv_j = [sb(f"qkv_j{n}", [128, T]) for n in range(NW)]
        yT = sb("yT", [128, T])

        iota_i = sb("iota_i", [128, E], mybir.dt.int32)
        iota_e = sb("iota_e", [128, E])
        score = sb("score", [128, NT, E])
        rest = sb("rest", [128, NT, E])
        rank = sb("rank", [128, NT, E])
        hot1 = sb("hot1", [128, NT, E])
        hot2 = sb("hot2", [128, NT, E])
        prob = sb("prob", [128, NT, E])
        top = [sb(f"top{n}", [128, NT]) for n in range(4)]
        diff = sb("diff", [128, NT])
        ratio = sb("ratio", [128, NT])
        p1 = sb("p1", [128, NT])
        p2 = sb("p2", [128, NT])
        euler = sb("euler", [128, NT])
        probT = sb("probT", [E, T])

        w12_nat = two("w12_nat", [128, H2 // 128, D])
        w3_nat = two("w3_nat", [128, H])
        w12_hi = sb("w12_hi", [128, E * H2], f32r)
        w12_lo = sb("w12_lo", [128, E * H2], f32r)
        w3_hi = sb("w3_hi", [128, E * H], f32r)
        w3_lo = sb("w3_lo", [128, E * H], f32r)
        h2_hi = two("h2_hi", [128, T], f32r)
        h2_lo = two("h2_lo", [128, T], f32r)
        act_h = [tk, uk] + kT
        pup = [tq, uq]
        hid_hi = v_hi + v_lo
        hid_lo = two("hid_lo", [128, T], f32r)
        out_sb = [t[:, :].rearrange("p (n d) -> p n d", d=D) for t in kvsum]

        bank = [ctx.enter_context(nc.psum_tensor(f"bank{n}", [128, 512], fp32)) for n in range(8)]

        names = """x_first x_rest small_in wqkv_in wgate_in wproj_in wmod_in 
            ident0 ident_ready consts selects cols_p cols_ready siluc modp setup_v biasp projp projj wsetup
            stats1_done meanvar1_done vareps1_done rstd1_done xn_done xnT_done hT_done hc_p z_p hc_done sg_done expz_done softplus_done shift_done
            sq_done var_p lnvar_done rstd2_done gm_p lngm_done invgm_done xh_done gate_done k_p v_p q_p
            tk_done uk_done k_done tq_done uq_done q_done vhi_done vlo_done ksum_done qk_done den_p lnden_done
            invden_done qn_done vrep_p kv_done kvsum_done qkvj_done y_p yT_done x2T_p x2_done
            cstats_done cmeanvar_done cvareps_done crstd_done cxn_done cxnT_done h2T_done h2hi_done h2lo_done
            score_p score_done route ratio_done prob_done probT_p probT_done prob_out prob_passed
            p_in0 p_in1 p_in2 p_in3 w12_in0 w12_in1 w3_in0 w3_in1 w12T_p w3T_p w12hi_done w12lo_done w3hi_done w3lo_done
            up_p silu_done pup_done hid_done hidhi_done hidlo_done down_p outT_done outT_p res_done stored""".split()
        s = {n: sem("s_" + n) for n in names}

        block = ctx.enter_context(nc.Block())

        PRIMED = {"x2T_p", "x2_done", "outT_done", "outT_p",
                  "res_done"}

        def prime(eng, *names):
            for name in names:
                eng.sem_inc(s[name], 1)

        def wait(eng, name, count):
            if isinstance(count, int) and count <= 0:
                return
            eng.wait_ge(s[name], count + 1 if name in PRIMED else count)

        def pipelined(eng, step, lead=True):
            if lead:
                step(-1, 1, False, True, False)
            step(0, 0, True, True, False)
            with eng.Fori(1, B - 2, 2) as b:
                step(b, 1, True, True, True)
                step(b + 1, 0, True, True, True)
            step(B - 1, 1, True, False, True)
            step(B, 0, False, False, True)

        def lagged(b, p, i, lag, has_back, has_old, M=M):
            if i >= lag:
                return [(b, p, i - lag)] if has_back else []
            return [(b - 1, 1 - p, M + i - lag)] if has_old else []

        def lagged_j(b, p, j, lag, has_back, has_old):
            return lagged(b, p, j, lag, has_back, has_old, DH)

        def batch(buf, b):
            return buf[:, bass.ds(b * T, T)]

        def tiles(buf, b):
            return buf[:, bass.ds(b * NT, NT), :]

        def column(buf2d, b):
            return buf2d[:, bass.ds(b, 1)]

        @block.sync
        def _(sp):
            x_t = x.rearrange("b (n p) d -> p (b n) d", p=128)
            out_t = out.rearrange("b (n p) d -> p (b n) d", p=128)
            sp.dma_start(x_all[:, 0:2 * NT, :], x_t[:, 0:2 * NT, :]).then_inc(s["x_first"], 16)
            sp.dma_start(wproj_sb[:, :], w_proj).then_inc(s["wproj_in"], 16)
            sp.dma_start(wmod_sb[:, :], wmod).then_inc(s["wmod_in"], 16)
            sp.wait_ge(s["small_in"], 16 * 7)
            sp.dma_start(wgate_sb[:, :], w_gate).then_inc(s["wgate_in"], 16)
            sp.dma_start(wqkv_sb[:, :], w_qkv).then_inc(s["wqkv_in"], 16)
            sp.dma_start(x_all[:, 2 * NT:, :], x_t[:, 2 * NT:, :]).then_inc(s["x_rest"], 16)

            def load_expert(e, q):
                wait(sp, "w12T_p", e - 1)
                wait(sp, "w3T_p", e - 1)
                sp.dma_start(w12_nat[q][:, :, :], w12[bass.ds(e, 1)].rearrange("e (a p) d -> p (e a) d", p=128))\
                    .then_inc(s[f"w12_in{q}"], 16)
                sp.dma_start(w3_nat[q][:, :], w3[bass.ds(e, 1)].rearrange("e d h -> d (e h)"))\
                    .then_inc(s[f"w3_in{q}"], 16)

            load_expert(0, 0)
            load_expert(1, 1)
            with sp.Fori(2, E - 1, 2) as e:
                load_expert(e, 0)
                load_expert(e + 1, 1)

            def spread(f):
                wait(sp, "probT_done", f + 1)
                sp.dma_start(prob_dram[bass.ds(f, 1)].rearrange("b e t -> (b e) t"), probT[:, :])\
                    .then_inc(s["prob_out"], 16)
                sp.wait_ge(s["prob_out"], 16 * (f + 1))
                sp.sem_inc(s["prob_passed"], 1)
                for e in range(E):
                    wait(sp, "pup_done", f * M + (e + 1 - RING) * KH)
                    sp.dma_start(batch(prob_row, e % RING),
                                 prob_dram[bass.ds(f, 1), e, :].to_broadcast([128, T])).then_inc(s[f"p_in{e % RING}"], 16)

            def store(b, p):
                wait(sp, "res_done", b + 1)
                sp.dma_start(out_t[:, bass.ds(b * NT, NT), :], out_sb[p]).then_inc(s["stored"], 16)

            spread(0)
            spread(1)
            with sp.Fori(2, B - 1, 2) as f:
                store(f - 2, 0)
                spread(f)
                store(f - 1, 1)
                spread(f + 1)
            store(B - 2, 0)
            store(B - 1, 1)
            sp.wait_ge(s["stored"], 16 * (B + 1))

        @block.gpsimd
        def _(pool):
            pool.memset(sel[:, :, :], 0.0).then_inc(s["ident0"], 1)
            pool.memset(ident[:, :], 0.0).then_inc(s["ident0"], 1)
            pool.memset(headsum[:, :], 1.0).then_inc(s["ident0"], 1)
            pool.wait_ge(s["ident0"], 3)
            pool.affine_select(out=sel[:, :, :].rearrange("p j (h i) -> p j h i", i=DH),
                               in_=sel[:, :, :].rearrange("p j (h i) -> p j h i", i=DH),
                               compare_op=ALU.not_equal, fill=1.0, base=0,
                               pattern=[[-1, DH], [-DH, HEADS], [0, DH]], channel_multiplier=1)\
                .then_inc(s["selects"], 1)
            pool.affine_select(out=ident[:, :], in_=ident[:, :], compare_op=ALU.not_equal, fill=1.0, base=0,
                               pattern=[[-1, 128]], channel_multiplier=1).then_inc(s["ident_ready"], 1)
            pool.memset(minus_half[:, :], -0.5).then_inc(s["consts"], 1)
            pool.memset(eps_tiles[:, :], EPS).then_inc(s["consts"], 1)
            pool.memset(euler[:, :], math.e).then_inc(s["consts"], 1)
            pool.memset(mean_w[:, :], 1.0 / D).then_inc(s["consts"], 1)
            hs = headsum[:, :].rearrange("p (h i) -> p h i", i=DH)
            pool.affine_select(out=hs, in_=hs, compare_op=ALU.is_ge, fill=0.0, base=0,
                               pattern=[[-DH, HEADS], [0, DH]], channel_multiplier=1).then_inc(s["selects"], 1)
            pool.wait_ge(s["selects"], 2)
            pool.affine_select(out=hs, in_=hs, compare_op=ALU.is_ge, fill=0.0, base=DH - 1,
                               pattern=[[DH, HEADS], [0, DH]], channel_multiplier=-1).then_inc(s["selects"], 1)
            pool.iota(iota_i[:, :], pattern=[[1, E]], base=0, channel_multiplier=0).then_inc(s["selects"], 1)

            def rstd_of(prefix, f, p):
                wait(pool, f"{prefix}meanvar_done", f + 1)
                wait(pool, f"{prefix}xn_done", f - 1)
                pool.tensor_tensor(vareps[p][:, :], meanvar[p][:, :, 1], eps_tiles[:, 0:NT], ALU.add)\
                    .then_inc(s[f"{prefix}vareps_done"], 1)
                wait(pool, f"{prefix}vareps_done", f + 1)
                pool.tensor_tensor(rstd[p][:, :], vareps[p][:, :], minus_half[:, 0:NT], ALU.pow)\
                    .then_inc(s[f"{prefix}rstd_done"], 1)

            pool.wait_ge(s["consts"], 4)

            def first_rstd_of(tokens, n):
                pool.wait_ge(s["meanvar1_done"], n)
                pool.tensor_tensor(first_vareps[:, tokens], first_meanvar[:, tokens, 1], eps_tiles[:, tokens], ALU.add)\
                    .then_inc(s["vareps1_done"], 1)
                pool.wait_ge(s["vareps1_done"], n)
                pool.tensor_tensor(first_rstd[:, tokens], first_vareps[:, tokens], minus_half[:, tokens], ALU.pow)\
                    .then_inc(s["rstd1_done"], 1)

            first_rstd_of(slice(0, 2 * NT), 1)

            def front_d(f, fp, i):
                if i == 1:
                    rstd_of("c", f, fp)
                if i == 11:
                    wait(pool, "route", f * LINKS + (DIFF + 1))
                    pool.tensor_tensor(ratio[:, :], euler[:, :], diff[:, :], ALU.pow).then_inc(s["ratio_done"], 1)

            def step_b(b, p, has_back, has_front, has_old):
                f, fp = b + 1, 1 - p
                for j in range(DH):
                    if j == 2 and has_back:
                        wait(pool, "ksum_done", b + 1)
                        wait(pool, "q_done", b + 1)
                        wait(pool, "den_p", b)
                        pool.tensor_tensor(qk[:, :], ksum[:, :], qT[p][:, :], ALU.mult).then_inc(s["qk_done"], 1)
                    if j == 4 and has_back:
                        wait(pool, "invden_done", b + 1)
                        pool.tensor_tensor(qn[p][:, :], qT[p][:, :], inv_den[:, :], ALU.mult)\
                            .then_inc(s["qn_done"], 1)
                    if j == 4 and has_front:
                        wait(pool, "rstd2_done", f + 1)
                        wait(pool, "q_p", f)
                        pool.tensor_tensor(xh[:, :], hc[:, :], rstd2[:, :], ALU.mult).then_inc(s["xh_done"], 1)
                    for pb, pp, pj in lagged_j(b, p, j, LAG_J, has_back, has_old):
                        wait(pool, "kvsum_done", pb * DH + (pj + 1))
                        wait(pool, "y_p", pb * DH + (pj + 1 - NW))
                        wait(pool, "qn_done", pb + 1)
                        pool.tensor_tensor(qkv_j[pj % NW][:, :], kvsum[pj % 2][:, :], qn[pp][:, :], ALU.mult)\
                            .then_inc(s["qkvj_done"], 1)
                    if j == 4 and has_front:
                        wait(pool, "invgm_done", f + 1)
                        wait(pool, "tq_done", f)
                        pool.tensor_tensor(gate[:, :], sg[:, :], inv_gm[:, :], ALU.mult).then_inc(s["gate_done"], 1)
                        if isinstance(f, int) and f == 0:
                            first_rstd_of(slice(2 * NT, B * NT), 2)
                    if not has_front:
                        for i in FRONT_D[j if has_back else DH + j]:
                            front_d(0, 0, i)

            pipelined(pool, step_b)

            def step_d(b, p, has_back, has_front, has_old):
                f, fp = b + 1, 1 - p
                for i in range(M):
                    for pb, pp, pi in lagged(b, p, i, LAG, has_back, has_old):
                        wait(pool, "silu_done", pb * M + (pi + 1))
                        wait(pool, "pup_done", pb * M + (pi + 1))
                        pool.tensor_tensor(act_h[pi % RING][:, :], act_h[pi % RING][:, :], pup[pi % 2][:, :], ALU.mult)\
                            .then_inc(s["hid_done"], 1)
                    if has_front:
                        front_d(f, fp, i)

            pipelined(pool, step_d, lead=False)

        @block.scalar
        def _(act):
            prime(act, "outT_done")
            act.dma_start(rows[G_:G_ + 1, :], ln_g.rearrange("(a d) -> a d", a=1)).then_inc(s["small_in"], 16)
            act.dma_start(rows[LB_:LB_ + 1, :], ln_b.rearrange("(a d) -> a d", a=1)).then_inc(s["small_in"], 16)
            act.dma_start(rows[BQ_:BQ_ + 3, :], b_qkv.rearrange("(a d) -> a d", a=3)).then_inc(s["small_in"], 16)
            act.dma_start(rows[BG_:BG_ + 1, :], b_gate.rearrange("(a d) -> a d", a=1)).then_inc(s["small_in"], 16)
            act.dma_start(rows[BP_:BP_ + 1, :], b_proj.rearrange("(a d) -> a d", a=1)).then_inc(s["small_in"], 16)
            act.dma_start(rows[C_:C_ + B, :], c).then_inc(s["small_in"], 16)
            act.dma_start(rows[GW_:GW_ + E, :], gate_w).then_inc(s["small_in"], 16)

            act.wait_ge(s["cols_ready"], 1)
            act.activation(silu_c[:, :], cols[:, C_:C_ + B], ACT.Silu).then_inc(s["siluc"], 1)
            act.wait_ge(s["projp"], 1)
            act.activation(proj_j[:, 0:DH // 2, :], bank[5][:, :].rearrange("p (b d) -> p b d", d=D), ACT.Copy)
            act.activation(proj_j[:, DH // 2:DH, :], bank[6][:, :].rearrange("p (b d) -> p b d", d=D), ACT.Copy)\
                .then_inc(s["projj"], 1)

            def prepare(e):
                wait(act, "w12T_p", e + 1)
                act.activation(w12_hi[:, bass.ds(e * H2, H2)], bank[3][:, :], ACT.Copy).then_inc(s["w12hi_done"], 1)
                wait(act, "w3T_p", e + 1)
                act.activation(w3_hi[:, bass.ds(e * H, H)], bank[4][:, 0:H], ACT.Copy)\
                    .then_inc(s["w3hi_done"], 1)

            def front_d(f, fp, i, to):
                if i == 5:
                    wait(act, "cxnT_done", f + 1)
                    wait(act, "h2lo_done", f - 1)
                    wait(act, "score_p", f - 1)
                    act.activation(hT[fp][:, :], to[:, :], ACT.Identity, bias=column(mod[:, SB, :], f),
                                   scale=column(mod[:, CB, :], f)).then_inc(s["h2T_done"], 1)
                if i == 8:
                    wait(act, "h2T_done", f + 1)
                    wait(act, "up_p", (f - 1) * M)
                    act.activation(h2_hi[fp][:, :], hT[fp][:, :], ACT.Copy).then_inc(s["h2hi_done"], 1)
                if i == 15:
                    wait(act, "probT_p", f + 1)
                    wait(act, "prob_out", 16 * f)
                    act.activation(probT[:, :], to[0:E, :], ACT.Copy).then_inc(s["probT_done"], 1)

            def step_b(b, p, has_back, has_front, has_old):
                f, fp = b + 1, 1 - p
                if has_front:
                    act.wait_ge(s["shift_done"], 1 if isinstance(f, int) and f < 2 else 2)
                    wait(act, "xnT_done", f - 1)
                    for t in range(NT):
                        last = act.activation(xn[fp][:, t, :], x_all[:, bass.ds(f * NT + t, 1), :], ACT.Identity,
                                              bias=column(first_shift, f * NT + t), scale=column(first_rstd, f * NT + t))
                    last.then_inc(s["xn_done"], 1)
                    act.wait_ge(s["wsetup"], 7)
                    wait(act, "xnT_done", f + 1)
                    wait(act, "z_p", f - 1)
                    act.activation(hT[fp][:, :], bank[0][:, :], ACT.Identity, bias=column(mod[:, SA, :], f),
                                   scale=column(mod[:, CA, :], f)).then_inc(s["hT_done"], 1)
                if has_front:
                    wait(act, "hc_p", f + 1)
                    wait(act, "xh_done", f)
                    act.activation(hc[:, :], bank[1][:, :], ACT.Copy).then_inc(s["hc_done"], 1)
                    wait(act, "var_p", f)
                    act.activation(sq[:, :], bank[1][:, :], ACT.Square).then_inc(s["sq_done"], 1)
                    if isinstance(f, int) and f == 0:
                        act.add_instruction(mybir.InstLoadActFuncSet(
                            name=nc.get_next_instruction_name(), act_func_set_id=LN_EXP_SET,
                            engine=mybir.EngineType.Activation))
                        act.wait_ge(s["wsetup"], 8)
                    wait(act, "z_p", f + 1)
                    act.activation(expz[:, :], bank[2][:, :], ACT.Exp, bias=minus_bg[:, :], scale=-1.0)\
                        .then_inc(s["expz_done"], 1)
                    wait(act, "expz_done", f + 1)
                    act.activation(expz[:, :], expz[:, :], ACT.Ln, bias=1.0).then_inc(s["softplus_done"], 1)
                if has_back:
                    wait(act, "den_p", b + 1)
                    act.activation(ln_den[:, :], bank[3][:, :], ACT.Ln, bias=eps_col[:, :]).then_inc(s["lnden_done"], 1)
                    wait(act, "lnden_done", b + 1)
                    wait(act, "qn_done", b)
                    act.activation(inv_den[:, :], ln_den[:, :], ACT.Exp, scale=-1.0).then_inc(s["invden_done"], 1)
                if has_front:
                    wait(act, "var_p", f + 1)
                    act.activation(ln_var[:, :], bank[1][:, :], ACT.Ln, bias=eps_col[:, :]).then_inc(s["lnvar_done"], 1)
                    wait(act, "softplus_done", f + 1)
                    wait(act, "gate_done", f)
                    act.activation(sg[:, :], expz[:, :], ACT.Exp, scale=-1.0).then_inc(s["sg_done"], 1)
                    wait(act, "lnvar_done", f + 1)
                    act.activation(rstd2[:, :], ln_var[:, :], ACT.Exp, scale=-0.5).then_inc(s["rstd2_done"], 1)
                if has_back:
                    prepare(b)
                if has_front:
                    wait(act, "gm_p", f + 1)
                    act.activation(ln_gm[:, :], bank[0][:, :], ACT.Ln, bias=eps_col[:, :]).then_inc(s["lngm_done"], 1)
                    wait(act, "lngm_done", f + 1)
                    act.activation(inv_gm[:, :], ln_gm[:, :], ACT.Exp, scale=-1.0).then_inc(s["invgm_done"], 1)
                if not has_front:
                    for i in range(6) if has_back else [M - 1]:
                        front_d(0, 0, i, bank[0])
                if has_old:
                    wait(act, "y_p", b * DH)
                    wait(act, "x2T_p", b - 1)
                    act.activation(yT[:, :], bank[7][:, :], ACT.Identity, bias=column(ga_bp, b - 1),
                                   scale=column(ga, b - 1)).then_inc(s["yT_done"], 1)
                if has_front:
                    act.wait_ge(s["setup_v"], 1)
                    wait(act, "v_p", f + 1)
                    wait(act, "vrep_p", f * DH - DH)
                    act.activation(v_hi[fp][:, :], bank[4][:, :], ACT.Identity, bias=bias_qkv[:, 2:3])\
                        .then_inc(s["vhi_done"], 1)
                if has_back and not has_front:
                    for i in range(6, M - 1):
                        front_d(0, 0, i, bank[0])

            pipelined(act, step_b)

            act.wait_ge(s["uk_done"], B)
            act.wait_ge(s["kv_done"], B * DH)
            act.wait_ge(s["vrep_p"], B * DH)

            def step_d(b, p, has_back, has_front, has_old):
                f, fp = b + 1, 1 - p
                for i in range(M):
                    for pb, pp, pi in lagged(b, p, i, LAG, has_back, has_old):
                        wait(act, "up_p", pb * M + (pi + 1))
                        wait(act, "hidlo_done", pb * M + (pi + 1 - RING))
                        act.activation(act_h[pi % RING][:, :], bank[pi % 2 * 2][:, :], ACT.Silu)\
                            .then_inc(s["silu_done"], 1)
                    for pb, pp, pi in lagged(b, p, i, LAG + 2, has_back, has_old):
                        wait(act, "hid_done", pb * M + (pi + 1))
                        wait(act, "down_p", pb * M + (pi + 1 - RING))
                        act.activation(hid_hi[pi % RING][:, :], act_h[pi % RING][:, :], ACT.Copy)\
                            .then_inc(s["hidhi_done"], 1)
                    if i == LAG + 4 and has_old:
                        wait(act, "down_p", b * M)
                        wait(act, "outT_p", b - 1)
                        act.activation(yT[:, :], bank[4 + (1 - p)][:, :], ACT.Copy, scale=column(gb, b - 1))\
                            .then_inc(s["outT_done"], 1)
                    if has_front:
                        front_d(f, fp, i, bank[6])

            pipelined(act, step_d, lead=False)

        @block.vector
        def _(dve):
            prime(dve, "x2_done", "res_done")
            def statistics(tokens):
                for t in tokens:
                    last = dve.bn_stats(first_stats[:, t, :], x_all[:, t, :])
                last.then_inc(s["stats1_done"], 1)
                dve.wait_ge(s["stats1_done"], 1 if tokens[0] == 0 else 2)
                for t in tokens:
                    last = dve.bn_aggr(first_meanvar[:, t, :], first_stats[:, t, :])
                last.then_inc(s["meanvar1_done"], 1)

            def shift(tokens, n):
                dve.wait_ge(s["rstd1_done"], n)
                dve.scalar_tensor_tensor(first_shift[:, tokens], first_meanvar[:, tokens, 0], -1.0,
                                         first_rstd[:, tokens], ALU.mult, ALU.mult).then_inc(s["shift_done"], 1)

            dve.wait_ge(s["x_first"], 16)
            statistics(range(0, 2 * NT))
            shift(slice(0, 2 * NT), 1)
            dve.memset(eps_col[:, :], EPS).then_inc(s["wsetup"], 1)
            dve.wait_ge(s["cols_p"], 1)
            dve.tensor_copy(cols[:, :], bank[0][:, 0:NROWS]).then_inc(s["cols_ready"], 1)
            dve.wait_ge(s["ident_ready"], 1)
            dve.tensor_scalar(centre[:, :], ident[:, :], -1.0 / D, 1.0, ALU.add, ALU.mult).then_inc(s["wsetup"], 1)
            dve.wait_ge(s["selects"], 4)
            dve.tensor_copy(sel_r[:, :, :], sel[:, :, :]).then_inc(s["wsetup"], 1)
            dve.tensor_copy(iota_e[:, :], iota_i[:, :]).then_inc(s["wsetup"], 1)
            dve.wait_ge(s["modp"], 1)
            dve.tensor_copy(mod[:, :, :], bank[1][:, 0:6 * B].rearrange("p (c b) -> p c b", b=B)).then_inc(s["wsetup"], 1)
            dve.wait_ge(s["wsetup"], 5)
            for ch in (CA, CB):
                dve.tensor_scalar(mod[:, ch, :], mod[:, ch, :], 1.0, None, ALU.add).then_inc(s["wsetup"], 1)
            dve.tensor_scalar(minus_bg[:, :], cols[:, BG_:BG_ + 1], -1.0, None, ALU.mult).then_inc(s["wsetup"], 1)
            g_raw = mod[:, GA:GB + 1:GB - GA, :]
            dve.tensor_scalar(g_sign[:, :, :], g_raw, 0.0, 2.0, ALU.is_ge, ALU.mult).then_inc(s["wsetup"], 1)
            dve.wait_ge(s["wsetup"], 9)
            dve.scalar_tensor_tensor(g_abs[:, :, :], g_sign[:, :, :], -1.0, g_raw, ALU.add, ALU.mult)\
                .then_inc(s["wsetup"], 1)
            dve.wait_ge(s["wsetup"], 10)
            dve.tensor_scalar(g_abs[:, :, :], g_abs[:, :, :], 0.25, None, ALU.max).then_inc(s["wsetup"], 1)
            dve.wait_ge(s["wsetup"], 11)
            dve.scalar_tensor_tensor(g_ab[:, :, :], g_sign[:, :, :], -1.0, g_abs[:, :, :], ALU.add, ALU.mult)\
                .then_inc(s["wsetup"], 1)
            dve.wait_ge(s["wsetup"], 12)
            dve.tensor_scalar(ga_bp[:, :], ga, cols[:, BP_:BP_ + 1], None, ALU.mult).then_inc(s["wsetup"], 1)
            dve.wait_ge(s["wqkv_in"], 16)
            dve.tensor_scalar(wqkv_g[:, :], wqkv_sb[:, :], cols[:, G_:G_ + 1], None, ALU.mult).then_inc(s["wsetup"], 1)
            dve.wait_ge(s["biasp"], 1)
            dve.tensor_tensor(bias_qkv[:, :], bank[4][:, 0:3], cols[:, BQ_:BQ_ + 3], ALU.add).then_inc(s["wsetup"], 1)
            dve.wait_ge(s["wsetup"], 15)
            dve.memset(stats[0][:, :, :], 0.0).then_inc(s["setup_v"], 1)
            dve.wait_ge(s["setup_v"], 1)

            def batch_stats(prefix, f, fp):
                for t in range(NT):
                    last = dve.bn_stats(stats[fp][:, t, :], x_all[:, bass.ds(f * NT + t, 1), :])
                last.then_inc(s[f"{prefix}stats_done"], 1)
                wait(dve, f"{prefix}stats_done", f + 1)
                wait(dve, f"{prefix}vareps_done", f - 1)
                dve.memset(spare[:, :], 0.0)
                for t in range(NT):
                    last = dve.bn_aggr(meanvar[fp][:, t, :], stats[fp][:, t, :])
                last.then_inc(s[f"{prefix}meanvar_done"], 1)

            def normalise(b, p, meanvar, rstd):
                for t in range(NT):
                    last = dve.tensor_scalar(xn[p][:, t, :], x_all[:, bass.ds(b * NT + t, 1), :],
                                             meanvar[:, t, 0:1], rstd[:, t:t + 1], ALU.subtract, ALU.mult)
                return last

            def prepare(e):
                w, w3 = bass.ds(e * H2, H2), bass.ds(e * H, H)
                wait(dve, "w12hi_done", e + 1)
                dve.tensor_tensor(w12_lo[:, w], bank[3][:, :], w12_hi[:, w].bitcast(fp32), ALU.subtract)\
                    .then_inc(s["w12lo_done"], 1)
                wait(dve, "w3hi_done", e + 1)
                dve.tensor_tensor(w3_lo[:, w3], bank[4][:, 0:H], w3_hi[:, w3].bitcast(fp32), ALU.subtract)\
                    .then_inc(s["w3lo_done"], 1)

            full = [128, NT, E]
            each = iota_e[:, :].unsqueeze(1).to_broadcast(full)

            def wide(t):
                return t[:, :].unsqueeze(2).to_broadcast(full)

            def route(f, first, ops):
                for n, op in enumerate(ops):
                    wait(dve, "route", f * LINKS + (first + n))
                    if first + n == DIFF + 1:
                        wait(dve, "ratio_done", f + 1)
                    op().then_inc(s["route"], 1)

            def first_max(scores, best, index, onehot):
                return [lambda: dve.tensor_reduce(best[:, :], scores[:, :, :], AX.X, ALU.max),
                        lambda: dve.tensor_tensor(rank[:, :, :], scores[:, :, :], wide(best), ALU.is_lt),
                        lambda: dve.scalar_tensor_tensor(rank[:, :, :], rank[:, :, :], float(E), each, ALU.mult,
                                                         ALU.add),
                        lambda: dve.tensor_reduce(index[:, :], rank[:, :, :], AX.X, ALU.min),
                        lambda: dve.tensor_tensor(onehot[:, :, :], each, wide(index), ALU.is_equal)]

            routing = first_max(score, top[0], top[1], hot1) \
                + [lambda: dve.scalar_tensor_tensor(rest[:, :, :], hot1[:, :, :], -3.0e38, score[:, :, :],
                                                    ALU.mult, ALU.add)] \
                + first_max(rest, top[2], top[3], hot2) \
                + [lambda: dve.tensor_tensor(diff[:, :], top[2][:, :], top[0][:, :], ALU.subtract),
                   lambda: dve.tensor_scalar(p2[:, :], ratio[:, :], 1.0, None, ALU.add),
                   lambda: dve.reciprocal(p1[:, :], p2[:, :]),
                   lambda: dve.tensor_tensor(p2[:, :], ratio[:, :], p1[:, :], ALU.mult),
                   lambda: dve.tensor_tensor(hot1[:, :, :], hot1[:, :, :], wide(p1), ALU.mult),
                   lambda: dve.tensor_tensor(hot2[:, :, :], hot2[:, :, :], wide(p2), ALU.mult),
                   lambda: dve.tensor_tensor(prob[:, :, :], hot1[:, :, :], hot2[:, :, :], ALU.add)]

            def front_d(f, fp, i, to):
                if i == 0:
                    batch_stats("c", f, fp)
                if i == 3:
                    wait(dve, "crstd_done", f + 1)
                    wait(dve, "cxnT_done", f - 1)
                    normalise(f, fp, meanvar[fp], rstd[fp]).then_inc(s["cxn_done"], 1)
                if i == 12:
                    wait(dve, "h2hi_done", f + 1)
                    wait(dve, "up_p", (f - 1) * M)
                    dve.tensor_tensor(h2_lo[fp][:, :], hT[fp][:, :], h2_hi[fp][:, :].bitcast(fp32),
                                      ALU.subtract).then_inc(s["h2lo_done"], 1)
                if i == 7:
                    wait(dve, "score_p", f + 1)
                    wait(dve, "route", f * LINKS)
                    dve.tensor_copy(score[:, :, :], to[:, 0:NT * E].rearrange("p (n e) -> p n e", e=E))\
                        .then_inc(s["score_done"], 1)
                    wait(dve, "score_done", f + 1)
                n = {7: (0, 2), 8: (2, 5), 9: (5, 8), 10: (8, 10), 11: (10, 12), 13: (12, 15), 14: (15, 18)}.get(i)
                if n:
                    route(f, n[0], routing[n[0]:n[1]])

            def step_b(b, p, has_back, has_front, has_old):
                f, fp = b + 1, 1 - p
                for j in range(DH):
                    if j == 0 and has_front and isinstance(f, int) and f == 0:
                        dve.wait_ge(s["x_rest"], 16)
                        statistics(range(2 * NT, B * NT))
                    for pb, pp, pj in lagged_j(b, p, j, LAG_J, has_back, has_old):
                        wait(dve, "vrep_p", pb * DH + (pj + 1))
                        dve.tensor_tensor(kv[pj % 2], bank[5 + pj % 2][:, :], kT[pp][:, :], ALU.mult)\
                            .then_inc(s["kv_done"], 1)
                        wait(dve, "kv_done", pb * DH + (pj + 1))
                        wait(dve, "qkvj_done", pb * DH + (pj + 1 - 2))
                        dve.tensor_tensor_scan(kvsum[pj % 2][:, :], kv[pj % 2], kv[pj % 2], 0.0,
                                               ALU.add, ALU.bypass).then_inc(s["kvsum_done"], 1)
                    if j == 0 and has_back:
                        wait(dve, "q_p", b + 1)
                        dve.scalar_tensor_tensor(tq[:, :], bank[2][:, :], bias_qkv[:, 0:1], gate[:, :],
                                                 ALU.add, ALU.mult).then_inc(s["tq_done"], 1)
                        wait(dve, "k_done", b + 1)
                        wait(dve, "qk_done", b)
                        dve.tensor_tensor_scan(ksum[:, :], kT[p][:, :], kT[p][:, :], 0.0, ALU.add, ALU.bypass)\
                            .then_inc(s["ksum_done"], 1)
                    if j == 1 and has_back:
                        wait(dve, "tq_done", b + 1)
                        dve.scalar_tensor_tensor(uq[:, :], tq[:, :], 0.0, tq[:, :], ALU.max, ALU.mult)\
                            .then_inc(s["uq_done"], 1)
                        wait(dve, "uq_done", b + 1)
                        wait(dve, "qn_done", b)
                        dve.tensor_scalar(qT[p][:, :], uq[:, :], EPS, None, ALU.add).then_inc(s["q_done"], 1)
                    if j == 5 and has_back:
                        prepare(b)
                        if isinstance(b, int) and b == 0:
                            shift(slice(2 * NT, B * NT), 2)
                    if j == 6 and has_front:
                        wait(dve, "k_p", f + 1)
                        wait(dve, "gate_done", f + 1)
                        dve.scalar_tensor_tensor(tk[:, :], bank[3][:, :], bias_qkv[:, 1:2], gate[:, :],
                                                 ALU.add, ALU.mult).then_inc(s["tk_done"], 1)
                        wait(dve, "tk_done", f + 1)
                        dve.scalar_tensor_tensor(uk[:, :], tk[:, :], 0.0, tk[:, :], ALU.max, ALU.mult)\
                            .then_inc(s["uk_done"], 1)
                    if j == 7 and has_front:
                        wait(dve, "vhi_done", f + 1)
                        dve.scalar_tensor_tensor(v_lo[fp][:, :], bank[4][:, :], bias_qkv[:, 2:3],
                                                 v_hi[fp][:, :].bitcast(fp32), ALU.add, ALU.subtract)\
                            .then_inc(s["vlo_done"], 1)
                        wait(dve, "uk_done", f + 1)
                        dve.tensor_scalar(kT[fp][:, :], uk[:, :], EPS, None, ALU.add).then_inc(s["k_done"], 1)
                    if j == 7 and has_old:
                        wait(dve, "x2T_p", b)
                        dve.tensor_tensor(tiles(x_all, b - 1), bank[1][:, :].rearrange("p (n d) -> p n d", d=D),
                                          tiles(x_all, b - 1), ALU.add).then_inc(s["x2_done"], 1)
                    if not has_front:
                        for i in FRONT_D[j if has_back else DH + j]:
                            front_d(0, 0, i, bank[0])

            pipelined(dve, step_b)

            wait(dve, "x2_done", B)

            dve.sem_inc(s["stored"], 16)
            wait(dve, "q_done", B)
            wait(dve, "qkvj_done", B * DH)

            def step_d(b, p, has_back, has_front, has_old):
                f, fp = b + 1, 1 - p
                for i in range(M):
                    for pb, pp, pi in lagged(b, p, i, LAG, has_back, has_old):
                        e = pi // KH
                        wait(dve, "up_p", pb * M + (pi + 1))
                        wait(dve, f"p_in{e % RING}", pb * 32 + 16 * (e // RING + 1))
                        wait(dve, "hid_done", pb * M + (pi + 1 - 2))
                        dve.tensor_tensor(pup[pi % 2][:, :], bank[pi % 2 * 2 + 1][:, :], batch(prob_row, e % RING),
                                          ALU.mult).then_inc(s["pup_done"], 1)
                    for pb, pp, pi in lagged(b, p, i, LAG + 3, has_back, has_old):
                        wait(dve, "hidhi_done", pb * M + (pi + 1))
                        wait(dve, "down_p", pb * M + (pi + 1 - 2))
                        dve.tensor_tensor(hid_lo[pi % 2][:, :], act_h[pi % RING][:, :],
                                          hid_hi[pi % RING][:, :].bitcast(fp32), ALU.subtract)\
                            .then_inc(s["hidlo_done"], 1)
                    if has_front:
                        front_d(f, fp, i, bank[6])
                    if i == LAG + 7 and has_old:
                        wait(dve, "outT_p", b)
                        dve.wait_ge(s["stored"], 16 * b)
                        dve.tensor_tensor(out_sb[1 - p], bank[7][:, :].rearrange("p (n d) -> p n d", d=D),
                                          tiles(x_all, b - 1), ALU.add).then_inc(s["res_done"], 1)

            pipelined(dve, step_d, lead=False)

        @block.tensor
        def _(pe):
            prime(pe, "x2T_p", "outT_p")
            pe.wait_ge(s["selects"], 1)
            pe.wait_ge(s["wproj_in"], 16)
            for j in range(DH):
                last = pe.matmul(bank[5 + j // 4][:, j % 4 * D:(j % 4 + 1) * D], sel[:, j, :], wproj_sb[:, :],
                                 start=True, stop=True)
            last.then_inc(s["projp"], 1)
            pe.wait_ge(s["small_in"], 16 * 7)
            pe.wait_ge(s["ident_ready"], 1)
            pe.transpose(bank[0][:, 0:NROWS], rows[:, :], ident[0:NROWS, 0:NROWS]).then_inc(s["cols_p"], 1)
            pe.wait_ge(s["siluc"], 1)
            pe.wait_ge(s["wmod_in"], 16)
            for ch in range(6):
                last = pe.matmul(bank[1][:, ch * B:(ch + 1) * B], wmod_sb[:, ch * D:(ch + 1) * D], silu_c[:, :],
                                 start=True, stop=True)
            last.then_inc(s["modp"], 1)

            def transposes(prefix, b, p, to):
                wait(pe, f"{prefix}xn_done", b + 1)
                for t in range(NT):
                    last = pe.transpose(to[:, t * 128:(t + 1) * 128], xn[p][:, t, :], ident[:, :])
                last.then_inc(s[f"{prefix}xnT_done"], 1)

            def v_columns(b, p, j):
                pe.wait_ge(s["projj"], 1)
                wait(pe, "vlo_done", b + 1)
                wait(pe, "kv_done", b * DH + (j + 1 - 2))
                pe.matmul(bank[5 + j % 2][:, :], sel_r[:, j, :], v_hi[p][:, :], start=True, stop=False)
                pe.matmul(bank[5 + j % 2][:, :], sel_r[:, j, :], v_lo[p][:, :], start=False, stop=True)\
                    .then_inc(s["vrep_p"], 1)

            def project(b, j):
                wait(pe, "qkvj_done", b * DH + (j + 1))
                if j == 0:
                    wait(pe, "yT_done", b)
                pe.matmul(bank[7][:, :], proj_j[:, j, :], qkv_j[j % NW][:, :], start=(j == 0), stop=(j == DH - 1))\
                    .then_inc(s["y_p"], 1)

            def prepare(e, q):
                wait(pe, f"w12_in{q}", 8 * (e - q) + 16)
                for a in range(H2 // 128):
                    last = pe.transpose(bank[3][:, a * 128:(a + 1) * 128], w12_nat[q][:, a, :], ident[:, :])
                last.then_inc(s["w12T_p"], 1)
                wait(pe, f"w3_in{q}", 8 * (e - q) + 16)
                for k in range(KH):
                    last = pe.transpose(bank[4][:, k * 128:(k + 1) * 128], w3_nat[q][:, k * 128:(k + 1) * 128],
                                        ident[:, :])
                last.then_inc(s["w3T_p"], 1)

            def front_d(f, fp, i, to):
                if i == 4:
                    wait(pe, "probT_done", f)
                    transposes("c", f, fp, to)
                if i == 6:
                    wait(pe, "h2T_done", f + 1)
                    for t in range(NT):
                        last = pe.matmul(to[:, t * E:(t + 1) * E], hT[fp][:, t * 128:(t + 1) * 128],
                                         cols[:, GW_:GW_ + E], start=True, stop=True)
                    last.then_inc(s["score_p"], 1)
                if i == 15:
                    wait(pe, "route", (f + 1) * LINKS)
                    for t in range(NT):
                        last = pe.transpose(to[0:E, t * 128:(t + 1) * 128], prob[:, t, :], ident[:, :])
                    last.then_inc(s["probT_p"], 1)

            def step_b(b, p, has_back, has_front, has_old):
                f, fp = b + 1, 1 - p
                for j in range(DH):
                    for pb, pp, pj in lagged_j(b, p, j, LAG_J - 1, has_back, has_old):
                        v_columns(pb, pp, pj)
                    if j == 1 and has_front:
                        wait(pe, "lngm_done", f)
                        transposes("", f, fp, bank[0])
                    if j == 3 and has_back:
                        wait(pe, "qk_done", b + 1)
                        wait(pe, "tk_done", b + 1)
                        pe.matmul(bank[3][:, :], headsum[:, :], qk[:, :], start=True, stop=True)\
                            .then_inc(s["den_p"], 1)
                    if j == 2 and has_front:
                        wait(pe, "hT_done", f + 1)
                        wait(pe, "x2_done", b - 1)
                        pe.matmul(bank[1][:, :], centre[:, :], hT[fp][:, :], start=True, stop=True)\
                            .then_inc(s["hc_p"], 1)
                        pe.wait_ge(s["wgate_in"], 16)
                        wait(pe, "tq_done", f)
                        pe.matmul(bank[2][:, :], wgate_sb[:, :], hT[fp][:, :], start=True, stop=True)\
                            .then_inc(s["z_p"], 1)
                        if isinstance(f, int) and f == 0:
                            pe.wait_ge(s["wqkv_in"], 16)
                            pe.wait_ge(s["cols_ready"], 1)
                            for ch in range(3):
                                last = pe.matmul(bank[4][:, ch:ch + 1], wqkv_sb[:, ch * D:(ch + 1) * D],
                                                 cols[:, LB_:LB_ + 1], start=True, stop=True)
                            last.then_inc(s["biasp"], 1)
                    if j == 4 and has_back:
                        wait(pe, "lnden_done", b + 1)
                        wait(pe, "vlo_done", b + 1)
                        prepare(b, p)
                    if j == 3 and has_front:
                        wait(pe, "sq_done", f + 1)
                        pe.matmul(bank[1][:, :], mean_w[:, :], sq[:, :], start=True, stop=True)\
                            .then_inc(s["var_p"], 1)
                    if j == 4 and has_front:
                        wait(pe, "sg_done", f + 1)
                        pe.matmul(bank[0][:, :], mean_w[:, :], sg[:, :], start=True, stop=True)\
                            .then_inc(s["gm_p"], 1)
                    if j == 5 and has_front:
                        pe.wait_ge(s["setup_v"], 1)
                        wait(pe, "xh_done", f + 1)
                        wait(pe, "w12lo_done", f)
                        pe.matmul(bank[3][:, :], wqkv_g[:, D:2 * D], xh[:, :], start=True, stop=True)\
                            .then_inc(s["k_p"], 1)
                        wait(pe, "w3lo_done", f)
                        pe.matmul(bank[4][:, :], wqkv_g[:, 2 * D:3 * D], xh[:, :], start=True, stop=True)\
                            .then_inc(s["v_p"], 1)
                    if j == 6 and has_front:
                        pe.matmul(bank[2][:, :], wqkv_g[:, 0:D], xh[:, :], start=True, stop=True)\
                            .then_inc(s["q_p"], 1)
                    if j == 6 and has_old:
                        wait(pe, "yT_done", b)
                        if has_front:
                            wait(pe, "lnvar_done", f + 1)
                        for t in range(NT):
                            last = pe.transpose(bank[1][:, t * 128:(t + 1) * 128], yT[:, t * 128:(t + 1) * 128],
                                                ident[:, :])
                        last.then_inc(s["x2T_p"], 1)
                    for pb, pp, pj in lagged_j(b, p, j, LAG_J + 2, has_back, has_old):
                        project(pb, pj)
                    if not has_front:
                        if has_back and j == 0:
                            wait(pe, "lngm_done", B)
                        for i in FRONT_D[j if has_back else DH + j]:
                            front_d(0, 0, i, bank[0])

            pipelined(pe, step_b)

            wait(pe, "lnden_done", B)
            wait(pe, "x2_done", B)
            wait(pe, "tk_done", B)
            wait(pe, "tq_done", B)

            wait(pe, "kv_done", B * DH)
            wait(pe, "yT_done", B)
            wait(pe, "vlo_done", B)
            def step_d(b, p, has_back, has_front, has_old):
                f, fp = b + 1, 1 - p
                for i in range(M):
                    for pb, pp, pi in lagged(b, p, i, LAG, has_back, has_old):
                        e, k = pi // KH, pi % KH
                        if pi == 0:
                            wait(pe, "probT_done", pb + 1)
                            wait(pe, "w12lo_done", E)
                            wait(pe, "w3lo_done", E)
                            wait(pe, "h2lo_done", pb + 1)
                        wait(pe, "silu_done", pb * M + (pi + 1 - 2))
                        wait(pe, "pup_done", pb * M + (pi + 1 - 2))
                        for half in range(2):
                            w = slice(e * H2 + half * H + k * 128, e * H2 + half * H + (k + 1) * 128)
                            o = bank[pi % 2 * 2 + half][:, :]
                            pe.matmul(o, w12_hi[:, w], h2_hi[pp][:, :], start=True, stop=False)
                            pe.matmul(o, w12_hi[:, w], h2_lo[pp][:, :], start=False, stop=False)
                            last = pe.matmul(o, w12_lo[:, w], h2_hi[pp][:, :], start=False, stop=True)
                        last.then_inc(s["up_p"], 1)
                    for pb, pp, pi in lagged(b, p, i, LAG + 4, has_back, has_old):
                        wait(pe, "hidlo_done", pb * M + (pi + 1))
                        if pi == 0:
                            wait(pe, "outT_done", pb - 1)
                        o = bank[4 + pp][:, :]
                        w = slice(pi * 128, (pi + 1) * 128)
                        pe.matmul(o, w3_hi[:, w], hid_hi[pi % RING][:, :], start=(pi == 0), stop=False)
                        pe.matmul(o, w3_lo[:, w], hid_hi[pi % RING][:, :], start=False, stop=False)
                        pe.matmul(o, w3_hi[:, w], hid_lo[pi % 2][:, :], start=False, stop=(pi == M - 1))\
                            .then_inc(s["down_p"], 1)
                    if i == LAG + 6 and has_old:
                        wait(pe, "outT_done", b)
                        wait(pe, "res_done", b - 1)
                        for t in range(NT):
                            last = pe.transpose(bank[7][:, t * 128:(t + 1) * 128], yT[:, t * 128:(t + 1) * 128],
                                                ident[:, :])
                        last.then_inc(s["outT_p"], 1)
                    if has_front:
                        front_d(f, fp, i, bank[6])

            pipelined(pe, step_d, lead=False)


_INS = ['L0_attn_x', 'L0_attn_ln_g', 'L0_attn_ln_b', 'L0_attn_W_qkv', 'L0_attn_b_qkv', 'L0_attn_W_gate', 'L0_attn_b_gate',
        'L0_attn_W_proj', 'L0_attn_b_proj', 'L0_ffn_w12', 'L0_ffn_w3', 'L0_ffn_gate_w', 'L0_c', 'L0_wmod']
_OUTS = [((8, 512, 128), 'float32')]


def kernel(**inputs):
    import numpy as _np
    import concourse.bacc as _bacc
    from concourse import mybir as _mybir
    from concourse.bass_utils import run_bass_kernel_spmd as _run

    nc = _bacc.Bacc("TRN2", target_bir_lowering=False, num_devices=1)
    arrays, args = {}, []
    for name in _INS:
        a = _np.ascontiguousarray(inputs[name])
        if a.dtype.kind in "iu":
            a = a.astype(_np.int64)
        arrays[f"in_{name}_dram"] = a
        args.append(nc.dram_tensor(f"in_{name}_dram", a.shape, _mybir.dt.from_np(a.dtype), kind="ExternalInput").ap())
    for i, (shape, dtype) in enumerate(_OUTS):
        dt = _mybir.dt.from_np(_np.dtype(dtype))
        args.append(nc.dram_tensor(f"out_{i}_dram", shape, dt, kind="ExternalOutput").ap())
    adaln_block(nc, *args)
    r = _run(nc, [arrays], core_ids=[0])
    got = tuple(r.results[0][f"out_{i}_dram"] for i in range(len(_OUTS)))
    return got[0]
```
